# Optimizing a Trainium2 kernel written in Bass

```python
import numpy as np
import jax
import jax.numpy as jnp

def _softmax(x, axis=-1):
    return jax.nn.softmax(x, axis=axis)

def _gelu(x):
    return jax.nn.gelu(x, approximate=True)

def _silu(x):
    return jax.nn.silu(x)

def _sigmoid(x):
    return jax.nn.sigmoid(x)

def _layernorm(x, axis=-1, eps=1e-05):
    m = jnp.mean(x, axis=axis, keepdims=True)
    v = jnp.var(x, axis=axis, keepdims=True)
    return (x - m) / jnp.sqrt(v + eps)

def _scatter_add(tgt, idx, src, axis=0):
    return tgt.at[idx].add(src)

def _segment_sum(src, seg, n):
    return jax.ops.segment_sum(src, seg, n)
kernel_name = 'mk_recurrent_d1_jaxref_r8_2b962f'

def setup_inputs(seed: int=0):
    np.random.seed(seed)
    _w = jnp.asarray

    def _L0_attn_setup():
        import jax, jax.numpy as jnp
        import numpy as np
        import math
        EPS = 1e-08
        B, S, D = (2, 256, 128)
        NH = 4
        DH = D // NH
        BLK = 4
        NQKV = D // BLK

        def _headwise(x, w):
            b, s, _ = x.shape
            xr = x.reshape(b, s, NQKV, BLK)
            y = jnp.einsum('bshi,hoi->bsho', xr, w)
            return y.reshape(b, s, -1)

        def _parallel_stabilized(q, k, v, ig, fg, eps=EPS):
            b, nh, s, dh = q.shape
            log_fg = jax.nn.log_sigmoid(fg)
            cs = jnp.concatenate([jnp.zeros((b, nh, 1, 1), q.dtype), jnp.cumsum(log_fg, axis=-2)], axis=-2)
            diff = cs - jnp.swapaxes(cs, -2, -1)
            ltr = jnp.tril(jnp.ones((s, s), dtype=bool))
            log_fg_mat = jnp.where(ltr[None, None], diff[:, :, 1:, 1:], -jnp.inf)
            log_D = log_fg_mat + jnp.swapaxes(ig, -2, -1)
            max_log_D = jnp.max(log_D, axis=-1, keepdims=True)
            D_mat = jnp.exp(log_D - max_log_D)
            qk = jnp.einsum('bnsd,bntd->bnst', q, k / math.sqrt(dh))
            C = qk * D_mat
            sum_C_abs = jnp.abs(jnp.sum(C, axis=-1, keepdims=True))
            normaliser = jnp.maximum(sum_C_abs, jnp.exp(-max_log_D))
            C_norm = C / (normaliser + eps)
            return jnp.einsum('bnst,bntd->bnsd', C_norm, v)

        def _multihead_layernorm(h, ln_w, eps=1e-05):
            mean = jnp.mean(h, axis=-1, keepdims=True)
            var = jnp.var(h, axis=-1, keepdims=True)
            hn = (h - mean) / jnp.sqrt(var + eps)
            gamma = (1.0 + ln_w).reshape(NH, DH)
            return hn * gamma[None, :, None, :]
        key = jax.random.key(seed)
        ks = jax.random.split(key, 8)
        std = math.sqrt(2.0 / (5.0 * BLK))
        x = jax.random.normal(ks[0], (B, S, D), dtype=jnp.float32)
        wq = jax.random.normal(ks[1], (NQKV, BLK, BLK), dtype=jnp.float32) * std
        wk = jax.random.normal(ks[2], (NQKV, BLK, BLK), dtype=jnp.float32) * std
        wv = jax.random.normal(ks[3], (NQKV, BLK, BLK), dtype=jnp.float32) * std
        gstd = math.sqrt(2.0 / (5.0 * 3 * D))
        wi = jax.random.normal(ks[4], (NH, 3 * D), dtype=jnp.float32) * gstd
        bi = jax.random.normal(ks[5], (NH,), dtype=jnp.float32)
        wf = jax.random.normal(ks[6], (NH, 3 * D), dtype=jnp.float32) * gstd
        bf = jnp.linspace(3.4, 6.0, NH, dtype=jnp.float32)
        ln_w = jnp.zeros((D,), dtype=jnp.float32)
        return {'x': x, 'wq': wq, 'wk': wk, 'wv': wv, 'wi': wi, 'bi': bi, 'wf': wf, 'bf': bf, 'ln_w': ln_w}
    _L0_attn_in = _L0_attn_setup()

    def _L0_ffn_setup():
        import jax, jax.numpy as jnp
        import numpy as np
        DIM = 128
        HIDDEN = 512
        E = 8
        B, S = (2, 512)
        key = jax.random.key(seed)
        ks = jax.random.split(key, 8)
        sd = 1.0 / np.sqrt(DIM)
        sh = 1.0 / np.sqrt(HIDDEN)
        return {'x': jax.random.normal(ks[0], (B, S, DIM), dtype=jnp.float32), 'router_w': jax.random.uniform(ks[1], (DIM, E), jnp.float32, -sd, sd), 'router_b': jax.random.uniform(ks[2], (E,), jnp.float32, -sd, sd), 'w1': jax.random.uniform(ks[3], (E, DIM, 2 * HIDDEN), jnp.float32, -sd, sd), 'b1': jax.random.uniform(ks[4], (E, 2 * HIDDEN), jnp.float32, -sd, sd), 'w2': jax.random.uniform(ks[5], (E, HIDDEN, DIM), jnp.float32, -sh, sh), 'b2': jax.random.uniform(ks[6], (E, DIM), jnp.float32, -sh, sh)}
    _L0_ffn_in = _L0_ffn_setup()
    _d = {'L0_attn_x': _L0_attn_in['x'], 'L0_attn_wq': _L0_attn_in['wq'], 'L0_attn_wk': _L0_attn_in['wk'], 'L0_attn_wv': _L0_attn_in['wv'], 'L0_attn_wi': _L0_attn_in['wi'], 'L0_attn_bi': _L0_attn_in['bi'], 'L0_attn_wf': _L0_attn_in['wf'], 'L0_attn_bf': _L0_attn_in['bf'], 'L0_attn_ln_w': _L0_attn_in['ln_w'], 'L0_ffn_router_w': _L0_ffn_in['router_w'], 'L0_ffn_router_b': _L0_ffn_in['router_b'], 'L0_ffn_w1': _L0_ffn_in['w1'], 'L0_ffn_b1': _L0_ffn_in['b1'], 'L0_ffn_w2': _L0_ffn_in['w2'], 'L0_ffn_b2': _L0_ffn_in['b2']}
    _x0 = _d['L0_attn_x']
    _d['L0_attn_x'] = jax.random.normal(jax.random.fold_in(jax.random.key(seed), 1), (16, 256, 128), dtype=_x0.dtype)
    del _x0
    return _d

def reference(L0_attn_x, L0_attn_wq, L0_attn_wk, L0_attn_wv, L0_attn_wi, L0_attn_bi, L0_attn_wf, L0_attn_bf, L0_attn_ln_w, L0_ffn_router_w, L0_ffn_router_b, L0_ffn_w1, L0_ffn_b1, L0_ffn_w2, L0_ffn_b2):

    def _L0_attn_ref(x, wq, wk, wv, wi, bi, wf, bf, ln_w):
        import jax, jax.numpy as jnp
        import numpy as np
        import math
        EPS = 1e-08
        B, S, D = (2, 256, 128)
        NH = 4
        DH = D // NH
        BLK = 4
        NQKV = D // BLK

        def _headwise(x, w):
            b, s, _ = x.shape
            xr = x.reshape(b, s, NQKV, BLK)
            y = jnp.einsum('bshi,hoi->bsho', xr, w)
            return y.reshape(b, s, -1)

        def _parallel_stabilized(q, k, v, ig, fg, eps=EPS):
            b, nh, s, dh = q.shape
            log_fg = jax.nn.log_sigmoid(fg)
            cs = jnp.concatenate([jnp.zeros((b, nh, 1, 1), q.dtype), jnp.cumsum(log_fg, axis=-2)], axis=-2)
            diff = cs - jnp.swapaxes(cs, -2, -1)
            ltr = jnp.tril(jnp.ones((s, s), dtype=bool))
            log_fg_mat = jnp.where(ltr[None, None], diff[:, :, 1:, 1:], -jnp.inf)
            log_D = log_fg_mat + jnp.swapaxes(ig, -2, -1)
            max_log_D = jnp.max(log_D, axis=-1, keepdims=True)
            D_mat = jnp.exp(log_D - max_log_D)
            qk = jnp.einsum('bnsd,bntd->bnst', q, k / math.sqrt(dh))
            C = qk * D_mat
            sum_C_abs = jnp.abs(jnp.sum(C, axis=-1, keepdims=True))
            normaliser = jnp.maximum(sum_C_abs, jnp.exp(-max_log_D))
            C_norm = C / (normaliser + eps)
            return jnp.einsum('bnst,bntd->bnsd', C_norm, v)

        def _multihead_layernorm(h, ln_w, eps=1e-05):
            mean = jnp.mean(h, axis=-1, keepdims=True)
            var = jnp.var(h, axis=-1, keepdims=True)
            hn = (h - mean) / jnp.sqrt(var + eps)
            gamma = (1.0 + ln_w).reshape(NH, DH)
            return hn * gamma[None, :, None, :]
        b, s, d = x.shape
        q = _headwise(x, wq).reshape(b, s, NH, DH).transpose(0, 2, 1, 3)
        k = _headwise(x, wk).reshape(b, s, NH, DH).transpose(0, 2, 1, 3)
        v = _headwise(x, wv).reshape(b, s, NH, DH).transpose(0, 2, 1, 3)
        gate_in = jnp.concatenate([x, x, x], axis=-1)
        ig = (gate_in @ wi.T + bi).transpose(0, 2, 1)[..., None]
        fg = (gate_in @ wf.T + bf).transpose(0, 2, 1)[..., None]
        h_tilde = _parallel_stabilized(q, k, v, ig, fg)
        h = _multihead_layernorm(h_tilde, ln_w)
        return h.transpose(0, 2, 1, 3).reshape(b, s, d)

    def _L0_ffn_ref(x, router_w, router_b, w1, b1, w2, b2):
        import jax, jax.numpy as jnp
        import numpy as np
        DIM = 128
        HIDDEN = 512
        E = 8
        B, S = (2, 512)
        logits = jnp.einsum('bsd,de->bse', x, router_w) + router_b
        probs = jax.nn.softmax(logits, axis=-1)
        top1 = jnp.argmax(probs, axis=-1)
        out = jnp.zeros_like(x)
        for i in range(E):
            h = jnp.einsum('bsd,df->bsf', x, w1[i]) + b1[i]
            a, g = jnp.split(h, 2, axis=-1)
            y = jnp.einsum('bsh,hd->bsd', a * jax.nn.sigmoid(g), w2[i]) + b2[i]
            out = out + jnp.where((top1 == i)[..., None], y, 0.0)
        return out
    x = L0_attn_x
    xn = _layernorm(x, axis=-1)
    s = _L0_attn_ref(xn, L0_attn_wq, L0_attn_wk, L0_attn_wv, L0_attn_wi, L0_attn_bi, L0_attn_wf, L0_attn_bf, L0_attn_ln_w)
    g = _silu(_L0_ffn_ref(xn, L0_ffn_router_w, L0_ffn_router_b, L0_ffn_w1, L0_ffn_b1, L0_ffn_w2, L0_ffn_b2))
    x = x + s * g
    return x

_drawn_inputs = setup_inputs


def setup_inputs(seed=0):
    import zlib

    import numpy as np

    out = dict(_drawn_inputs(seed))
    spreads = {'L0_attn_ln_w': (0.0, 0.8)}
    factors = {'L0_attn_bi': 8.0,
     'L0_attn_wf': 8.0,
     'L0_attn_bf': 2.699,
     'L0_ffn_b1': 6.952,
     'L0_ffn_b2': 4.356}
    for name, (base, spread) in spreads.items():
        noise = np.random.default_rng([zlib.crc32(name.encode()), seed]).standard_normal(out[name].shape)
        drawn = base * np.exp(spread * noise) if base else spread * noise
        out[name] = jnp.asarray(drawn.astype(out[name].dtype))
    for name, factor in factors.items():
        out[name] = (out[name] * factor).astype(out[name].dtype)
    return out
```

```python
from contextlib import ExitStack

import concourse.bass as bass
from concourse import mybir

F32 = mybir.dt.float32
F32R = mybir.dt.float32r
BF16 = mybir.dt.bfloat16
I32 = mybir.dt.int32
ALU = mybir.AluOpType
ACT = mybir.ActivationFunctionType
AX = mybir.AxisListType

P = 128


def mlstm_moe_block(nc, x, wq, wk, wv, wi, bi, wf, bf, ln_w, router_w, router_b, w1, b1, w2, b2, out):
    B, S, D = x.shape
    NTOK = B * S
    T = NTOK // P
    NH = bi.shape[0]
    DH = D // NH
    DA = DH + 1
    E = w1.shape[0]
    H2 = w1.shape[2]
    HID = H2 // 2
    HC = HID // P
    R = B * NH
    NBLK = T + E - 1
    NX = 4
    CH = 3
    assert NBLK % CH == 0 and S == 2 * P and D == P and R == 64
    NCH = NBLK // CH
    XG = 4
    TG = T // XG
    LG = 2
    TL = T // LG
    BA = 9
    GROUPS = [(0, 4), (4, 4), (8, 4), (12, 2), (14, 2)]
    NG = len(GROUPS)
    GT = 8
    EPS_LN = 1e-5
    EPS_N = 1e-8
    GW = R - NH
    BIG = 3.0e38

    xs_dram = nc.dram_tensor("xs_sorted", (NBLK * P, D), F32).ap()
    ys_dram = nc.dram_tensor("ys_sorted", (NBLK * P, D), F32).ap()
    x_t = x.rearrange("b (k p) d -> p (b k) d", p=P)
    out_t = out.rearrange("b (k p) d -> p (b k) d", p=P)

    ctx = ExitStack()
    with ctx:
        def sb(name, shape, dt=F32):
            return ctx.enter_context(nc.sbuf_tensor(name, shape, dt))

        def sem(name):
            return ctx.enter_context(nc.semaphore(name))

        x_sb = sb("x_sb", [P, T, D])
        xn = sb("xn", [P, T, D])
        yg = xn
        xnT = sb("xnT", [P, NTOK])
        u_all = sb("u_all", [P, T, NH, DA])
        w1_sb = sb("w1_sb", [P, E * H2])
        w2_sb = sb("w2_sb", [P, E * HC * D])
        xs_sb = sb("xs_sb", [P, NX, CH, D])
        ys_sb = sb("ys_sb", [P, 2, CH, D])
        ident = sb("ident", [P, P])
        tril = sb("tril", [P, P], BF16)
        ones_bf = sb("ones_bf", [P, P], BF16)
        onesrow = sb("onesrow", [1, S])
        zeros = sb("zeros", [P, S])
        block4 = sb("block4", [P, P])
        head_mask = sb("head_mask", [P, NH, DA])
        pick_f = sb("pick_f", [P, R])
        pick = sb("pick", [P, R], F32R)
        desc8 = sb("desc8", [P, E])
        blk_start = sb("blk_start", [P, NBLK])
        row_i = sb("row_i", [P, 1], I32)
        row_m = sb("row_m", [P, 1], I32)
        row_e = sb("row_e", [P, 1])
        nat = sb("nat", [P, 3, 4])
        natbd = sb("natbd", [P, 3, P])
        wbd = sb("wbd", [P, 3, P])
        vmean = sb("vmean", [P, NH])
        wvk = sb("wvk", [P, 2, P])
        gates_raw = sb("gates_raw", [2 * NH, 3 * D])
        gates_w = sb("gates_w", [2 * NH, D])
        gate_cols = sb("gate_cols", [P, GW + P])
        gate_bias = sb("gate_bias", [1, 2 * R])
        rw_sb = sb("rw_sb", [P, E])
        rb_sb = sb("rb_sb", [P, E])
        gamma = sb("gamma", [P, D])
        b_parts = sb("b_parts", [P, H2 + D], BF16)
        stats = sb("stats", [P, T, 6])
        mv = sb("mv", [P, T, 2])
        NR = 64
        veps = sb("veps", [P, NR])
        ra = sb("ra", [P, NR])
        rb_ = sb("rb_", [P, NR])
        ry = sb("ry", [P, NR])
        ry2 = sb("ry2", [P, NR])
        rstd = sb("rstd", [P, T])
        nmr = sb("nmr", [P, T])
        lg = sb("lg", [P, T, E])
        r1 = sb("r1", [P, T, E])
        rmax = sb("rmax", [P, T])
        oh = sb("oh", [P, E, T], BF16)
        cnt = sb("cnt", [P, E, T])
        csum = sb("csum", [P, E, T])
        pos3 = sb("pos3", [P, E, T])
        ecount = sb("ecount", [P, E])
        ecount_i = sb("ecount_i", [P, E], I32)
        epad_i = sb("epad_i", [P, E], I32)
        epad = sb("epad", [P, E])
        eend = sb("eend", [P, E])
        edelta = sb("edelta", [P, E])
        posf = sb("posf", [P, T])
        pos = sb("pos", [P, T], I32)
        bcmp = sb("bcmp", [P, NBLK, E])
        bexp = sb("bexp", [P, NBLK])
        bexp_i = sb("bexp_i", [P, NBLK], I32)
        bhot = sb("bhot", [P, NBLK], BF16)
        bhot_x = sb("bhot_x", [P, NBLK, P], BF16)
        ig = sb("ig", [R, S])
        fg = sb("fg", [R, S])
        ga = sb("ga", [R, S])
        gb = sb("gb", [R, S])
        gc = sb("gc", [R, S])
        lf = sb("lf", [R, S])
        fsum = sb("fsum", [R, S])
        gg = sb("gg", [R, S])
        mm = sb("mm", [R, S])
        nm = sb("nm", [R, S])
        nm2 = sb("nm2", [P, S], F32R)
        eo_row = sb("eo_row", [R, P])
        w_row = sb("w_row", [R, P])
        fl_row = sb("fl_row", [R, S])
        tm = sb("tm", [P, 6, R])
        qm = sb("qm", [P, 2, NH, S])
        q1 = sb("q1", [P, 2, P])
        kT = sb("kT", [P, 2, S])
        va = sb("va", [P, 2, 2, NH, DA])
        vw = sb("vw", [P, 2, NH, DA])
        kt = sb("kt", [P, 2, P])
        dm = sb("dm", [P, 2, 2, NH, P])
        cm = sb("cm", [P, 2, 2, NH, P])
        st = sb("st", [P, 2, NH, DA])
        ot = sb("ot", [P, NH, DA])
        sq = cm[:, 1, :, :, :].rearrange("p k h s -> p (k h s)").rearrange("p (t h d) -> p t h d", t=GT, h=NH)
        ssum = sb("ssum", [P, GT * NH])
        den = sb("den", [P, GT * NH])
        rden = sb("rden", [P, GT * NH])
        coef = sb("coef", [P, GT * NH])
        xsT = sb("xsT", [P, 2, P])
        th = dm[:, 0, :, :, :].rearrange("p k h s -> p k (h s)")
        uT = dm[:, 1, :, :, :]
        uu = cm[:, 0, :, :, :].rearrange("p k h s -> p k (h s)")
        yt = w1_sb[:, 0:T * D].rearrange("p (t d) -> p t d", d=D)
        b_f = dm[0:E, :, :, :, :].rearrange("p a k h s -> p (a k h s)")[:, 0:H2 + D]
        b_r = cm[0:E, :, :, :, :].rearrange("p a k h s -> p (a k h s)")[:, 0:H2 + D]

        bank = [ctx.enter_context(nc.psum_tensor(f"bank{i}", [P, 512], F32)) for i in range(8)]

        s_x = [sem(f"s_x{i}") for i in range(XG)]
        s_small = sem("s_small")
        s_const = sem("s_const")
        s_bp = sem("s_bp")
        s_xna = sem("s_xna")
        s_rs = sem("s_rs")
        s_ig = sem("s_ig")
        s_zero = sem("s_zero")
        s_fill = sem("s_fill")
        s_w1 = sem("s_w1")
        s_w2 = sem("s_w2")
        s_chain = sem("s_chain")
        s_nat = sem("s_nat")
        s_wT = sem("s_wT")
        s_wbd = sem("s_wbd")
        s_gw = sem("s_gw")
        s_xn = sem("s_xn")
        s_xT = sem("s_xT")
        s_xTe = sem("s_xTe")
        s_lg = sem("s_lg")
        s_gp = sem("s_gp")
        s_oh = sem("s_oh")
        s_cnt = sem("s_cnt")
        s_pos = sem("s_pos")
        s_scat = sem("s_scat")
        s_bexp = sem("s_bexp")
        s_bhot = sem("s_bhot")
        s_abs = sem("s_abs")
        s_u = sem("s_u")
        s_w = sem("s_w")
        s_ln = sem("s_ln")
        s_mm = sem("s_mm")
        s_rows = sem("s_rows")
        s_tmp = sem("s_tmp")
        s_tm = sem("s_tm")
        s_qkp = sem("s_qkp")
        s_qke = sem("s_qke")
        s_vp = sem("s_vp")
        s_ve = sem("s_ve")
        s_ve2 = sem("s_ve2")
        s_vw = sem("s_vw")
        s_mb = sem("s_mb")
        s_dm = sem("s_dm")
        s_dsel = sem("s_dsel")
        s_sc = sem("s_sc")
        s_cm = sem("s_cm")
        s_stp = sem("s_stp")
        s_st = sem("s_st")
        s_o = sem("s_o")
        s_oe = sem("s_oe")
        s_ones = sem("s_ones")
        s_xs = [sem(f"s_xs{i}") for i in range(NX)]
        s_xsp = sem("s_xsp")
        s_xse = sem("s_xse")
        s_h = sem("s_h")
        s_th = sem("s_th")
        s_uu = sem("s_uu")
        s_utp = sem("s_utp")
        s_ute = sem("s_ute")
        s_yp = sem("s_yp")
        s_ye = sem("s_ye")
        s_yst = [sem(f"s_yst{i}") for i in range(2)]
        s_yg = [sem(f"s_yg{i}") for i in range(NG)]
        s_norm = sem("s_norm")
        s_yt = sem("s_yt")
        s_fin = sem("s_fin")
        s_out = sem("s_out")

        NSMALL = 12
        block = ctx.enter_context(nc.Block())

        @block.sync
        def _(sp):
            for i in range(XG):
                sp.dma_start(x_sb[:, i * TG:(i + 1) * TG, :], x_t[:, i * TG:(i + 1) * TG, :]).then_inc(s_x[i], 16)
            for e in range(E):
                sp.dma_start(w1_sb[:, e * H2:(e + 1) * H2], w1[e]).then_inc(s_w1, 16)
            sp.dma_start(w2_sb[:, :].rearrange("p (e c d) -> p e c d", e=E, c=HC),
                         w2.rearrange("e (c p) d -> p e c d", p=P)).then_inc(s_w2, 16)
            sp.wait_ge(s_zero, 1)
            sp.dma_start(xs_dram.rearrange("(n p) d -> p n d", p=P),
                         zeros[:, 0:D].unsqueeze(1).to_broadcast([P, NBLK, D])).then_inc(s_fill, 16)

            def store(c):
                sp.wait_ge(s_ye, CH * (c + 1))
                sp.dma_start(ys_dram[c * CH * P:(c + 1) * CH * P, :].rearrange("(n p) d -> p n d", p=P),
                             ys_sb[:, c % 2, :, :]).then_inc(s_yst[c % 2], 16)

            sp.wait_ge(s_scat, 16 * T)
            for c in range(NCH):
                if c >= NX:
                    sp.wait_ge(s_xsp, (c - NX + 1) * CH)
                sp.dma_start(xs_sb[:, c % NX, :, :],
                             xs_dram[c * CH * P:(c + 1) * CH * P, :].rearrange("(n p) d -> p n d", p=P)).then_inc(s_xs[c % NX], 16)
                if c >= NX - 1:
                    store(c - NX + 1)
            for c in range(NCH - NX + 1, NCH):
                store(c)
            for g, (b0, nb) in enumerate(GROUPS):
                ts = slice(2 * b0, 2 * (b0 + nb))
                sp.wait_ge(s_fin, g + 1)
                sp.dma_start(out_t[:, ts, :], yt[:, ts, :]).then_inc(s_out, 16)
            sp.wait_ge(s_out, 16 * NG)

        @block.gpsimd
        def _(pool):
            pool.memset(zeros[:, :], 0.0).then_inc(s_zero, 1)
            pool.memset(ident[:, :], 0.0).then_inc(s_const, 1)
            pool.memset(block4[:, :], 1.0).then_inc(s_const, 1)
            pool.memset(head_mask[:, :, :], 1.0).then_inc(s_const, 1)
            pool.memset(pick_f[:, :], 0.0).then_inc(s_const, 1)
            pool.memset(tril[:, :], 1.0).then_inc(s_const, 1)
            pool.wait_ge(s_const, 5)
            pool.affine_select(out=ident[:, :], in_=ident[:, :], compare_op=ALU.not_equal, fill=1.0,
                               base=0, pattern=[[-1, P]], channel_multiplier=1).then_inc(s_const, 1)
            b4 = block4[:, :].rearrange("p (g o) -> p g o", o=4)
            pool.affine_select(out=b4, in_=b4, compare_op=ALU.is_ge, fill=0.0,
                               base=0, pattern=[[-4, P // 4], [0, 4]], channel_multiplier=1).then_inc(s_const, 1)
            pool.affine_select(out=head_mask[:, :, :], in_=head_mask[:, :, :], compare_op=ALU.is_ge, fill=0.0,
                               base=0, pattern=[[-DH, NH], [0, DA]], channel_multiplier=1).then_inc(s_const, 1)
            pool.affine_select(out=pick_f[:, :], in_=pick_f[:, :], compare_op=ALU.not_equal, fill=1.0,
                               base=0, pattern=[[-1, R]], channel_multiplier=1).then_inc(s_const, 1)
            pool.affine_select(out=tril[:, :], in_=tril[:, :], compare_op=ALU.is_ge, fill=0.0,
                               base=-1, pattern=[[1, P]], channel_multiplier=-1).then_inc(s_const, 1)
            pool.wait_ge(s_const, 10)
            pool.affine_select(out=b4, in_=b4, compare_op=ALU.is_ge, fill=0.0,
                               base=3, pattern=[[4, P // 4], [0, 4]], channel_multiplier=-1).then_inc(s_const, 1)
            pool.affine_select(out=head_mask[:, :, :], in_=head_mask[:, :, :], compare_op=ALU.is_ge, fill=0.0,
                               base=DH - 1, pattern=[[DH, NH], [0, DA]], channel_multiplier=-1).then_inc(s_const, 1)
            pool.affine_select(out=pick_f[:, :], in_=pick_f[:, :], compare_op=ALU.not_equal, fill=1.0,
                               base=-R, pattern=[[-1, R]], channel_multiplier=1).then_inc(s_const, 1)
            pool.memset(ones_bf[:, :], 1.0).then_inc(s_const, 1)
            pool.memset(onesrow[:, :], 1.0).then_inc(s_const, 1)
            pool.iota(desc8[:, :], [[-1, E]], base=E, channel_multiplier=0,
                      allow_small_or_imprecise_dtypes=True).then_inc(s_const, 1)
            pool.iota(blk_start[:, :], [[P, NBLK]], base=0, channel_multiplier=0,
                      allow_small_or_imprecise_dtypes=True).then_inc(s_const, 1)
            pool.iota(row_i[:, :], [[0, 1]], base=0, channel_multiplier=1).then_inc(s_const, 1)
            pool.memset(va[:, :, :, :, DH:DA], 1.0).then_inc(s_ones, 1)
            pool.memset(qm[:, :, :, :], 0.0).then_inc(s_ones, 1)

            pool.wait_ge(s_small, 16 * NSMALL)
            pool.memset(b_parts[:, :], 0.0).then_inc(s_bp, 1)
            pool.wait_ge(s_bp, 1)
            pool.tensor_copy(b_parts[0:E, :], b_f).then_inc(s_bp, 1)
            pool.wait_ge(s_bp, 2)
            pool.tensor_tensor(b_r, b_f, b_parts[0:E, :], ALU.subtract).then_inc(s_bp, 1)
            pool.wait_ge(s_bp, 3)
            pool.tensor_copy(b_parts[32:32 + E, :], b_r).then_inc(s_bp, 1)
            pool.wait_ge(s_bp, 4)
            pool.tensor_copy(b_f, b_parts[32:32 + E, :]).then_inc(s_bp, 1)
            pool.wait_ge(s_bp, 5)
            pool.tensor_tensor(b_r, b_r, b_f, ALU.subtract).then_inc(s_bp, 1)
            pool.wait_ge(s_bp, 6)
            pool.tensor_copy(b_parts[64:64 + E, :], b_r).then_inc(s_bp, 1)
            pool.wait_ge(s_bp, 7)

            def batch_masks(b):
                pool.wait_ge(s_ve, b + 1)
                pool.wait_ge(s_tm, 1)
                if b >= 2:
                    pool.wait_ge(s_stp, b - 1)
                pool.tensor_tensor(vw[:, b % 2, :, :], va[:, b % 2, 0, :, :],
                                   tm[:, 3, NH * b:NH * (b + 1)].unsqueeze(2).to_broadcast([P, NH, DA]),
                                   ALU.mult).then_inc(s_vw, 1)
                for k in range(2):
                    pool.wait_ge(s_dm, 2 * b + k + 1)
                    d = dm[:, b % 2, k, :, :]
                    pool.affine_select(out=d, in_=d, compare_op=ALU.is_ge, fill=0.0, base=0,
                                       pattern=[[0, NH], [1, P]], channel_multiplier=-1).then_inc(s_dsel, 1)

            for b in range(BA):
                batch_masks(b)
                if b == 1:
                    pool.wait_ge(s_fill, 16)
                    pool.wait_ge(s_pos, 1)
                if b >= 1:
                    for t in range((b - 1) * T // (BA - 1), b * T // (BA - 1)):
                        pool.indirect_dma_start(xs_dram, bass.IndirectOffsetOnAxis(ap=pos[:, t:t + 1], axis=0),
                                                xn[:, t, :], None).then_inc(s_scat, 16)
            batch_masks(BA)
            pool.wait_ge(s_yst[0], 16 * ((NCH + 1) // 2))
            pool.wait_ge(s_yst[1], 16 * (NCH // 2))
            for b in range(BA, B):
                for t in range((b - BA) * T // (B - BA), (b - BA + 1) * T // (B - BA)):
                    g = [2 * b0 <= t < 2 * (b0 + nb) for b0, nb in GROUPS].index(True)
                    pool.indirect_dma_start(yg[:, t, :], None, ys_dram,
                                            bass.IndirectOffsetOnAxis(ap=pos[:, t:t + 1], axis=0))\
                        .then_inc(s_yg[g], 16)
                if b + 1 < B:
                    batch_masks(b + 1)

        @block.scalar
        def _(act):
            for n, w in enumerate((wq, wk, wv)):
                act.dma_start(nat[:, n, :], w.rearrange("h o i -> (h o) i")).then_inc(s_small, 16)
            act.dma_start(rw_sb[:, :], router_w).then_inc(s_small, 16)
            act.dma_start(gates_raw[0:NH, :], wi).then_inc(s_small, 16)
            act.dma_start(gates_raw[NH:2 * NH, :], wf).then_inc(s_small, 16)
            for n, v in enumerate((bf, bi)):
                act.dma_start(gate_bias[0:1, n * R:(n + 1) * R].rearrange("p (b h) -> p b h", h=NH),
                              v.partition_broadcast(B).unsqueeze(0)).then_inc(s_small, 16)
            act.dma_start(rb_sb[:, :], router_b.partition_broadcast(P)).then_inc(s_small, 16)
            act.dma_start(gamma[:, :], ln_w.partition_broadcast(P)).then_inc(s_small, 16)
            act.dma_start(b_f[:, 0:H2], b1).then_inc(s_small, 16)
            act.dma_start(b_f[:, H2:H2 + D], b2).then_inc(s_small, 16)
            for g in range(LG):
                act.wait_ge(s_rs, g + 1)
                for t in range(g * TL + 1, (g + 1) * TL, 2):
                    act.activation(xn[:, t, :], x_sb[:, t, :], ACT.Identity, scale=rstd[:, t:t + 1],
                                   bias=nmr[:, t:t + 1]).then_inc(s_xna, 1)
                    if t % 4 == 3 and t // 4 >= 1:
                        q = t // 4 - 1
                        act.wait_ge(s_xT, q + 1)
                        act.activation(xnT[:, q * 512:(q + 1) * 512], bank[q % 2][:, :], ACT.Copy).then_inc(s_xTe, 1)
            q = T // 4 - 1
            act.wait_ge(s_xT, q + 1)
            act.activation(xnT[:, q * 512:(q + 1) * 512], bank[q % 2][:, :], ACT.Copy).then_inc(s_xTe, 1)
            act.wait_ge(s_gp, 1)
            act.activation(ga[:, :], bank[6][0:R, 0:S], ACT.Abs).then_inc(s_abs, 1)
            act.wait_ge(s_abs, 1)
            act.activation(gb[:, :], ga[:, :], ACT.Exp, scale=-1.0).then_inc(s_u, 1)
            act.activation(ig[:, :], bank[6][R:2 * R, 0:S], ACT.Copy).then_inc(s_ig, 1)
            act.wait_ge(s_w, 1)
            act.activation(lf[:, :], gc[:, :], ACT.Ln).then_inc(s_ln, 1)
            act.wait_ge(s_mm, 2)
            act.activation(w_row[:, :], gg[:, 0:P], ACT.Exp, bias=nm[:, P - 1:P]).then_inc(s_rows, 1)
            act.activation(eo_row[:, :], mm[:, P:S], ACT.Exp, scale=-1.0, bias=mm[:, P - 1:P]).then_inc(s_rows, 1)
            act.activation(fl_row[:, :], ga[:, :], ACT.Exp, scale=-1.0).then_inc(s_rows, 1)
            def evac_qk(b):
                act.wait_ge(s_qkp, b + 1)
                if b >= 2:
                    act.wait_ge(s_o, b - 1)
                act.activation(kT[:, b % 2, :], bank[0][:, S:2 * S], ACT.Copy)
                for h in range(NH):
                    hs = slice(h * DH, (h + 1) * DH)
                    act.activation(qm[hs, b % 2, h, :], bank[0][hs, 0:S], ACT.Copy)
                act.activation(q1[:, b % 2, :], bank[0][:, P:S], ACT.Copy).then_inc(s_qke, 1)

            def decay(b):
                act.wait_ge(s_mb, b + 1)
                act.wait_ge(s_tm, 1)
                if b >= 2:
                    act.wait_ge(s_cm, 2 * (b - 1))
                for k in range(2):
                    for h in range(NH):
                        src = bank[2 + h // 2][:, (h % 2) * S + k * P:(h % 2) * S + (k + 1) * P]
                        last = act.activation(dm[:, b % 2, k, h, :], src, ACT.Exp,
                                              bias=tm[:, k, NH * b + h:NH * b + h + 1])
                    last.then_inc(s_dm, 1)

            def attention(b0, b1_, finish={}):
                evac_qk(b0)
                decay(b0)
                for b in range(b0, b1_):
                    if b + 1 < b1_:
                        evac_qk(b + 1)
                        decay(b + 1)
                    if b in finish:
                        tanh_y(finish[b])

            act.wait_ge(s_ones, 2)
            act.wait_ge(s_bp, 7)
            attention(0, BA)
            act.wait_ge(s_bhot, 1)
            act.activation(bhot_x[:, :, :], bhot[:, :].unsqueeze(2).to_broadcast([P, NBLK, P]), ACT.Copy).then_inc(s_bexp, 1)

            def glu(j):
                act.wait_ge(s_h, j + 1)
                if j >= 2:
                    act.wait_ge(s_uu, j - 1)
                act.activation(th[:, j % 2, :], bank[2 * (j % 2) + 1][:, :], ACT.Tanh, scale=0.5).then_inc(s_th, 1)

            def prodT(j):
                act.wait_ge(s_utp, j + 1)
                if j >= 2:
                    act.wait_ge(s_yp, j - 1)
                act.activation(uT[:, j % 2, :, :], bank[5][:, :], ACT.Copy, scale=0.5).then_inc(s_ute, 1)

            for j in range(NBLK + 1):
                if j < NBLK:
                    glu(j)
                if j >= 1:
                    prodT(j - 1)

            def tanh_y(g):
                b0, nb = GROUPS[g]
                ts = slice(2 * b0, 2 * (b0 + nb))
                act.wait_ge(s_yg[g], 16 * 2 * nb)
                act.activation(yt[:, ts, :], yg[:, ts, :], ACT.Tanh, scale=0.5).then_inc(s_yt, 1)

            attention(BA, B, {11: 0, 13: 1, 15: 2})
            for g in range(3, NG):
                tanh_y(g)

        @block.vector
        def _(dve):
            chain = [0]

            def link(ins):
                chain[0] += 1
                ins.then_inc(s_chain, 1)
                dve.wait_ge(s_chain, chain[0])

            def rsqrt(v, n):
                a, b, y, y2 = ra[:, 0:n], rb_[:, 0:n], ry[:, 0:n], ry2[:, 0:n]
                link(dve.tensor_scalar(a.bitcast(I32), v.bitcast(I32), 1, None, ALU.logical_shift_right))
                link(dve.tensor_scalar(y.bitcast(I32), a.bitcast(I32), -1.0, float(0x5F3759DF), ALU.mult, ALU.add))
                for _ in range(3):
                    link(dve.tensor_tensor(a, y, y, ALU.mult))
                    link(dve.scalar_tensor_tensor(b, a, -0.5, v, ALU.mult, ALU.mult))
                    link(dve.scalar_tensor_tensor(y2, b, 1.5, y, ALU.add, ALU.mult))
                    y, y2 = y2, y
                return y

            for g in range(LG):
                for t in range(g * TL, (g + 1) * TL):
                    if t % TG == 0:
                        dve.wait_ge(s_x[t // TG], 16)
                    last = dve.bn_stats(stats[:, t, :], x_sb[:, t, :])
                link(last)
                for t in range(g * TL, (g + 1) * TL):
                    last = dve.bn_aggr(mv[:, t, :], stats[:, t, :])
                link(last)
                gs = slice(g * TL, (g + 1) * TL)
                link(dve.tensor_scalar(veps[:, 0:TL], mv[:, gs, 1], EPS_LN, None, ALU.add))
                y = rsqrt(veps[:, 0:TL], TL)
                link(dve.tensor_copy(rstd[:, gs], y))
                dve.scalar_tensor_tensor(nmr[:, gs], mv[:, gs, 0], -1.0, rstd[:, gs], ALU.mult, ALU.mult).then_inc(s_rs, 1)
                dve.wait_ge(s_rs, g + 1)
                for t in range(g * TL, (g + 1) * TL, 2):
                    dve.tensor_scalar(xn[:, t, :], x_sb[:, t, :], rstd[:, t:t + 1], nmr[:, t:t + 1],
                                      ALU.mult, ALU.add).then_inc(s_xn, 1)
                if g == 0:
                    dve.wait_ge(s_small, 16 * NSMALL)
                    dve.wait_ge(s_const, 18)
                    for n in range(3):
                        dve.tensor_tensor(natbd[:, n, :].rearrange("p (g i) -> p g i", i=4),
                                          block4[:, :].rearrange("p (g i) -> p g i", i=4),
                                          nat[:, n, :].unsqueeze(1).to_broadcast([P, P // 4, 4]),
                                          ALU.mult).then_inc(s_nat, 1)
                    link(dve.tensor_tensor(gates_w[:, :], gates_raw[:, 0:D], gates_raw[:, D:2 * D], ALU.add))
                    dve.tensor_tensor(gates_raw[:, 0:D], gates_w[:, :], gates_raw[:, 2 * D:3 * D], ALU.add).then_inc(s_nat, 1)
                    dve.memset(gate_cols[:, :], 0.0).then_inc(s_chain, 1)
                    chain[0] += 1
                    dve.tensor_copy(pick[:, :], pick_f[:, :]).then_inc(s_nat, 1)
                    dve.tensor_scalar(gamma[:, :], gamma[:, :], 1.0, None, ALU.add).then_inc(s_chain, 1)
                    chain[0] += 1
                    dve.tensor_scalar(row_m[:, :], row_i[:, :], 31, None, ALU.bitwise_and).then_inc(s_chain, 1)
                    chain[0] += 1
                    dve.wait_ge(s_chain, chain[0])
                    dve.tensor_copy(row_e[:, :], row_m[:, :]).then_inc(s_chain, 1)
                    chain[0] += 1
                    dve.wait_ge(s_wT, 1)
                    link(dve.tensor_copy(wbd[:, :, :], bank[4][:, 0:3 * P].rearrange("p (n m) -> p n m", n=3)))
                    link(dve.tensor_copy(gate_cols[:, GW + R:GW + R + NH], bank[4][:, 3 * P:3 * P + NH]))
                    link(dve.tensor_copy(gate_cols[:, GW:GW + NH], bank[4][:, 3 * P + NH:3 * P + 2 * NH]))
                    link(dve.tensor_scalar(wvk[:, 1, :], wbd[:, 1, :], float(DH) ** -0.5, None, ALU.mult))
                    link(dve.tensor_reduce(vmean[:, :], wbd[:, 2, :].rearrange("p (h d) -> p h d", h=NH), AX.X, ALU.add))
                    link(dve.tensor_scalar(vmean[:, :], vmean[:, :], -1.0 / DH, None, ALU.mult))
                    dve.tensor_tensor(wvk[:, 0, :].rearrange("p (h d) -> p h d", h=NH),
                                      wbd[:, 2, :].rearrange("p (h d) -> p h d", h=NH),
                                      vmean[:, :].unsqueeze(2).to_broadcast([P, NH, DH]), ALU.add).then_inc(s_wbd, 1)

            dve.wait_ge(s_lg, 1)
            link(dve.tensor_tensor(lg[:, :, :], bank[2][:, 0:T * E].rearrange("p (t e) -> p t e", e=E),
                                   rb_sb[:, :].unsqueeze(1).to_broadcast([P, T, E]), ALU.add))
            link(dve.tensor_reduce(rmax[:, :], lg[:, :, :], AX.X, ALU.max))
            link(dve.tensor_tensor(r1[:, :, :], lg[:, :, :], rmax[:, :].unsqueeze(2).to_broadcast([P, T, E]), ALU.is_equal))
            link(dve.tensor_tensor(lg[:, :, :], r1[:, :, :], desc8[:, :].unsqueeze(1).to_broadcast([P, T, E]), ALU.mult))
            link(dve.tensor_reduce(rmax[:, :], lg[:, :, :], AX.X, ALU.max))
            dve.tensor_tensor(oh[:, :, :].rearrange("p e t -> p t e"), rmax[:, :].unsqueeze(2).to_broadcast([P, T, E]),
                              desc8[:, :].unsqueeze(1).to_broadcast([P, T, E]), ALU.is_equal).then_inc(s_oh, 1)
            dve.wait_ge(s_u, 1)
            link(dve.tensor_scalar(gc[:, :], gb[:, :], 1.0, None, ALU.add))
            dve.scalar_tensor_tensor(gb[:, :], gc[:, :], -1.0, gb[:, :], ALU.add, ALU.subtract).then_inc(s_w, 1)
            dve.wait_ge(s_cnt, 1)
            link(dve.tensor_copy(cnt[:, :, :], bank[3][:, 0:E * T].rearrange("p (e t) -> p e t", e=E)))
            link(dve.tensor_copy(pos3[:, :, :], bank[3][:, E * T:2 * E * T].rearrange("p (e t) -> p e t", e=E)))
            dve.wait_ge(s_ln, 1)
            dve.wait_ge(s_w, 1)
            link(dve.tensor_tensor(gc[:, :], gb[:, :], lf[:, :], ALU.subtract))
            link(dve.scalar_tensor_tensor(lf[:, :], bank[6][0:R, 0:S], 0.0, gc[:, :], ALU.min, ALU.add))
            link(dve.tensor_tensor_scan(fsum[:, :], lf[:, :], zeros[0:R, :], 0.0, ALU.add, ALU.add))
            dve.wait_ge(s_ig, 1)
            link(dve.tensor_tensor(gg[:, :], ig[:, :], fsum[:, :], ALU.subtract))
            link(dve.tensor_tensor_scan(mm[:, :], gg[:, :], gg[:, :], -BIG, ALU.max, ALU.max))
            dve.tensor_tensor(ga[:, :], fsum[:, :], mm[:, :], ALU.add).then_inc(s_mm, 1)
            link(dve.tensor_scalar(nm[:, :], mm[:, :], -1.0, None, ALU.mult))
            link(dve.tensor_copy(nm2[0:R, :], nm[:, :]))
            dve.tensor_tensor(nm2[R:2 * R, :], nm[:, :], nm2[0:R, :].bitcast(F32), ALU.subtract).then_inc(s_mm, 1)
            dve.wait_ge(s_tmp, 1)
            dve.tensor_copy(tm[:, :, :], bank[7][:, 0:6 * R].rearrange("p (n r) -> p n r", n=6)).then_inc(s_tm, 1)
            dve.wait_ge(s_tm, 1)
            dve.wait_ge(s_ones, 2)
            dve.wait_ge(s_bp, 7)

            def routing(part):
                flat = "p e t -> p (e t)"
                if part == 0:
                    link(dve.tensor_tensor_scan(csum[:, :, :].rearrange(flat), cnt[:, :, :].rearrange(flat),
                                                zeros[:, 0:E * T], 0.0, ALU.add, ALU.add))
                    link(dve.tensor_reduce(ecount[:, :], cnt[:, :, :], AX.X, ALU.add))
                if part == 1:
                    link(dve.tensor_scalar(ecount_i[:, :], ecount[:, :], float(P - 1), None, ALU.add))
                    link(dve.tensor_scalar(epad_i[:, :], ecount_i[:, :], 7, 7, ALU.logical_shift_right, ALU.logical_shift_left))
                    link(dve.tensor_copy(epad[:, :], epad_i[:, :]))
                    link(dve.tensor_tensor_scan(eend[:, :], epad[:, :], zeros[:, 0:E], 0.0, ALU.add, ALU.add))
                    link(dve.tensor_tensor(edelta[:, :], eend[:, :], epad[:, :], ALU.subtract))
                    link(dve.tensor_tensor(edelta[:, :], edelta[:, :], csum[:, :, T - 1], ALU.subtract))
                    link(dve.tensor_tensor(edelta[:, :], edelta[:, :], ecount[:, :], ALU.add))
                    link(dve.tensor_tensor(csum[:, :, :], csum[:, :, :], cnt[:, :, :], ALU.subtract))
                    link(dve.tensor_tensor(csum[:, :, :], csum[:, :, :], edelta[:, :].unsqueeze(2).to_broadcast([P, E, T]), ALU.add))
                    link(dve.tensor_tensor(pos3[:, :, :], pos3[:, :, :], csum[:, :, :], ALU.add))
                    link(dve.tensor_tensor(pos3[:, :, :], pos3[:, :, :], oh[:, :, :], ALU.mult))
                    link(dve.tensor_reduce(posf[:, :], pos3[:, :, :].rearrange("p e t -> p t e"), AX.X, ALU.add))
                    dve.tensor_copy(pos[:, :], posf[:, :]).then_inc(s_pos, 1)
                if part == 2:
                    link(dve.tensor_tensor(bcmp[:, :, :], blk_start[:, :].unsqueeze(2).to_broadcast([P, NBLK, E]),
                                           eend[:, :].unsqueeze(1).to_broadcast([P, NBLK, E]), ALU.is_ge))
                    link(dve.tensor_reduce(bexp[:, :], bcmp[:, :, :], AX.X, ALU.add))
                    link(dve.tensor_scalar(bexp[:, :], bexp[:, :], float(E - 1), None, ALU.min))
                    link(dve.tensor_copy(bexp_i[:, :], bexp[:, :]))
                    dve.tensor_scalar(bhot[:, :], bexp[:, :], row_e[:, :], None, ALU.is_equal).then_inc(s_bhot, 1)
    
            def evac_v(b):
                dve.wait_ge(s_vp, b + 1)
                if b >= 2:
                    dve.wait_ge(s_o, b - 1)
                    dve.wait_ge(s_vw, b - 1)
                dve.tensor_copy(va[:, b % 2, :, :, 0:DH],
                                bank[1][:, :].rearrange("p (k h d) -> p k h d", k=2, d=DH)[:, :, 0:NH, :]).then_inc(s_ve, 1)
                dve.tensor_copy(kt[:, b % 2, :], bank[1][:, P:2 * P]).then_inc(s_ve2, 1)

            def scores(b):
                for k in range(2):
                    dve.wait_ge(s_sc, 2 * b + k + 1)
                    dve.wait_ge(s_dsel, 2 * b + k + 1)
                    if b >= 2:
                        dve.wait_ge(s_o, b - 1)
                    dve.tensor_tensor(cm[:, b % 2, k, :, :], dm[:, b % 2, k, :, :],
                                      bank[4 + k][:, :].rearrange("p (h s) -> p h s", h=NH), ALU.mult).then_inc(s_cm, 1)

            def state(b):
                dve.wait_ge(s_stp, b + 1)
                if b >= 2:
                    dve.wait_ge(s_o, b - 1)
                dve.tensor_tensor(st[:, b % 2, :, :], head_mask[:, :, :],
                                  bank[6][:, 0:NH * DA].rearrange("p (h d) -> p h d", h=NH), ALU.mult).then_inc(s_st, 1)

            def outputs(b):
                dve.wait_ge(s_o, b + 1)
                hd = "p (h d) -> p h d"
                n = NH * DA
                dve.tensor_copy(u_all[:, 2 * b, :, :], bank[7][:, 0:n].rearrange(hd, h=NH))
                link(dve.tensor_tensor(ot[:, :, :], bank[7][:, 2 * n:3 * n].rearrange(hd, h=NH),
                                       tm[:, 2, NH * b:NH * (b + 1)].unsqueeze(2).to_broadcast([P, NH, DA]), ALU.mult))
                dve.tensor_tensor(u_all[:, 2 * b + 1, :, :], ot[:, :, :], bank[7][:, n:2 * n].rearrange(hd, h=NH),
                                  ALU.add).then_inc(s_oe, 1)

            def attention(b0, b1_):
                evac_v(b0)
                for b in range(b0, b1_):
                    state(b)
                    scores(b)
                    if b + 1 < b1_:
                        evac_v(b + 1)
                    outputs(b)
                    if b in (0, 1, 2):
                        routing(b)
                    for step, g, part in {11: [("n", 2, 0), ("n", 2, 1), ("f", 0, 0)], 12: [("n", 2, 2), ("n", 2, 3)],
                                          13: [("n", 3, 0), ("n", 3, 1), ("f", 1, 0)],
                                          14: [("n", 3, 2), ("n", 3, 3)]}.get(b, []):
                        if step == "n":
                            normalise(g, part)
                        else:
                            finish(g)

            def normalise(g, part):
                b0, nb = GROUPS[g]
                nt = 2 * nb
                n = nt * NH
                uv = u_all[:, 2 * b0:2 * b0 + nt, :, 0:DH]
                rs = u_all[:, 2 * b0:2 * b0 + nt, :, DH]
                dn = den[:, 0:n].rearrange("p (t h) -> p t h", h=NH)
                rd = rden[:, 0:n].rearrange("p (t h) -> p t h", h=NH)
                if part == 0:
                    dve.wait_ge(s_oe, b0 + nb)
                    link(dve.tensor_tensor(sq[:, 0:nt, :, :], uv, uv, ALU.mult))
                    link(dve.tensor_reduce(ssum[:, 0:n], sq[:, 0:nt, :, :], AX.X, ALU.add))
                if part == 1:
                    link(dve.tensor_scalar(rd, rs, -1.0, None, ALU.mult))
                    link(dve.tensor_tensor(dn, rd, rs, ALU.max))
                    fl = tm[:, 4:6, b0 * NH:(b0 + nb) * NH].rearrange("p k (b h) -> p b k h", h=NH)
                    d4 = den[:, 0:n].rearrange("p (b k h) -> p b k h", k=2, h=NH)
                    link(dve.tensor_tensor(d4, d4, fl, ALU.max))
                    link(dve.tensor_scalar(den[:, 0:n], den[:, 0:n], EPS_N, None, ALU.add))
                    link(dve.reciprocal(rden[:, 0:n], den[:, 0:n]))
                    link(dve.scalar_tensor_tensor(ssum[:, 0:n], ssum[:, 0:n], 1.0 / DH, rden[:, 0:n], ALU.mult, ALU.mult))
                    link(dve.tensor_tensor(ssum[:, 0:n], ssum[:, 0:n], rden[:, 0:n], ALU.mult))
                    link(dve.tensor_scalar(veps[:, 0:n], ssum[:, 0:n], EPS_LN, None, ALU.add))
                if part == 2:
                    y = rsqrt(veps[:, 0:n], n)
                    link(dve.scalar_tensor_tensor(coef[:, 0:n], y, 0.5, rden[:, 0:n], ALU.mult, ALU.mult))
                if part == 3:
                    link(dve.tensor_tensor(sq[:, 0:nt, :, :], uv,
                                           coef[:, 0:n].rearrange("p (t h) -> p t h", h=NH).unsqueeze(3).to_broadcast([P, nt, NH, DH]), ALU.mult))
                    link(dve.tensor_tensor(uv, sq[:, 0:nt, :, :],
                                           gamma[:, :].rearrange("p (h d) -> p h d", h=NH).unsqueeze(1).to_broadcast([P, nt, NH, DH]), ALU.mult))

            def finish(g):
                b0, nb = GROUPS[g]
                ts = slice(2 * b0, 2 * (b0 + nb))
                y = yt[:, ts, :]
                hd = "p t (h d) -> p t h d"
                dve.wait_ge(s_yt, g + 1)
                link(dve.scalar_tensor_tensor(y, y, 1.0, yg[:, ts, :], ALU.add, ALU.mult))
                link(dve.tensor_tensor(y.rearrange(hd, h=NH), y.rearrange(hd, h=NH), u_all[:, ts, :, 0:DH], ALU.mult))
                dve.tensor_tensor(y, y, x_sb[:, ts, :], ALU.add).then_inc(s_fin, 1)

            attention(0, BA)

            def evac_xs(j):
                dve.wait_ge(s_xsp, j + 1)
                if j >= 2:
                    dve.wait_ge(s_h, j - 1)
                dve.tensor_copy(xsT[:, j % 2, :], bank[4][:, 0:P]).then_inc(s_xse, 1)

            def product(j):
                dve.wait_ge(s_th, j + 1)
                if j >= 2:
                    dve.wait_ge(s_utp, j - 1)
                dve.scalar_tensor_tensor(uu[:, j % 2, :], th[:, j % 2, :], 1.0, bank[2 * (j % 2)][:, :],
                                         ALU.add, ALU.mult).then_inc(s_uu, 1)

            def evac_y(j):
                dve.wait_ge(s_yp, j + 1)
                if j >= 2 * CH and j % CH == 0:
                    dve.wait_ge(s_yst[j // CH % 2], 16 * (j // CH // 2))
                dve.tensor_copy(ys_sb[:, (j // CH) % 2, j % CH, :], bank[6][:, 0:D]).then_inc(s_ye, 1)

            evac_xs(0)
            for j in range(NBLK + 2):
                if j + 1 < NBLK:
                    evac_xs(j + 1)
                if j < NBLK:
                    product(j)
                if j >= 2:
                    evac_y(j - 2)
                if 4 <= j < 20 and j % 2 == 0:
                    normalise((j - 4) // 8, (j - 4) // 2 % 4)

            attention(BA, B)
            for part in range(4):
                normalise(4, part)
            for g in range(2, NG):
                finish(g)

        @block.tensor
        def _(pe):
            def transposes(q):
                pe.wait_ge(s_xn, 2 * (q + 1))
                pe.wait_ge(s_xna, 2 * (q + 1))
                if q >= 2:
                    pe.wait_ge(s_xTe, q - 1)
                for i in range(4):
                    last = pe.transpose(bank[q % 2][:, i * P:(i + 1) * P], xn[:, 4 * q + i, :], ident[:, :])
                last.then_inc(s_xT, 1)

            def logits(q):
                pe.wait_ge(s_xTe, q + 1)
                for t in range(4 * q, 4 * q + 4):
                    last = pe.matmul(bank[2][:, t * E:(t + 1) * E], xnT[:, t * P:(t + 1) * P], rw_sb[:, :],
                                     start=True, stop=True)
                if q == T // 4 - 1:
                    last.then_inc(s_lg, 1)

            def gates(b):
                pe.matmul(bank[6][:, 0:S], gate_cols[:, GW - NH * b:GW - NH * b + P], xnT[:, b * S:(b + 1) * S],
                          start=(b == 0), stop=False)

            pe.wait_ge(s_const, 18)
            for q in range(T // 4):
                transposes(q)
                if q == 0:
                    pe.wait_ge(s_nat, 5)
                    for n in range(3):
                        pe.transpose(bank[4][:, n * P:(n + 1) * P], natbd[:, n, :], ident[:, :])
                    pe.transpose(bank[4][:, 3 * P:3 * P + 2 * NH], gates_raw[:, 0:D], ident[0:2 * NH, 0:2 * NH]).then_inc(s_wT, 1)
                if q >= 1:
                    logits(q - 1)
                if q == T // 8:
                    pe.wait_ge(s_wbd, 1)
                    for b in range(2 * q):
                        gates(b)
                elif q > T // 8:
                    gates(2 * q - 2)
                    gates(2 * q - 1)
            logits(T // 4 - 1)
            gates(B - 2)
            gates(B - 1)
            pe.matmul(bank[6][:, 0:S], gate_bias[0:1, :], onesrow[0:1, :], start=False, stop=True).then_inc(s_gp, 1)
            pe.wait_ge(s_oh, 1)
            ohf = oh[:, :, :].rearrange("p e t -> p (e t)")
            pe.matmul(bank[3][:, 0:E * T], ones_bf[:, :], ohf, start=True, stop=True)
            pe.matmul(bank[3][:, E * T:2 * E * T], tril[:, :], ohf, start=True, stop=True).then_inc(s_cnt, 1)
            pe.wait_ge(s_mm, 2)
            pe.wait_ge(s_rows, 3)
            idr = ident[0:R, 0:R]
            for n, v in enumerate((gg[:, 0:P], gg[:, P:S], eo_row[:, :], w_row[:, :], fl_row[:, 0:P], fl_row[:, P:S])):
                last = pe.transpose(bank[7][:, n * R:(n + 1) * R], v, idr)
            last.then_inc(s_tmp, 1)

            def project(b):
                xb = xnT[:, b * S:(b + 1) * S]
                if b >= 1:
                    pe.wait_ge(s_qke, b)
                pe.matmul(bank[0][:, 0:S], wbd[:, 0, :], xb, start=True, stop=True)
                pe.matmul(bank[0][:, S:2 * S], wvk[:, 1, :], xb, start=True, stop=True).then_inc(s_qkp, 1)
                if b >= 1:
                    pe.wait_ge(s_ve2, b)
                wv_k = wvk[:, :, :].rearrange("p n m -> p (n m)")
                pe.matmul(bank[1][:, 0:2 * P], xnT[:, b * S:b * S + P], wv_k, start=True, stop=True)
                pe.matmul(bank[1][:, 2 * P:3 * P], xnT[:, b * S + P:(b + 1) * S], wvk[:, 0, :], start=True, stop=True).then_inc(s_vp, 1)
                if b >= 1:
                    pe.wait_ge(s_dm, 2 * b)
                for h in range(NH):
                    r = NH * b + h
                    last = pe.matmul(bank[2 + h // 2][:, (h % 2) * S:(h % 2 + 1) * S],
                                     pick[:, r:r + 1].to_broadcast([P, P]), nm2[:, :], start=True, stop=True)
                last.then_inc(s_mb, 1)

            def attention(b0, b1_):
                project(b0)
                for b in range(b0, b1_):
                    pe.wait_ge(s_qke, b + 1)
                    if b >= 1:
                        pe.wait_ge(s_cm, 2 * b)
                    for k in range(2):
                        pe.matmul(bank[4 + k][:, :], kT[:, b % 2, k * P:(k + 1) * P],
                                  qm[:, b % 2, :, k * P:(k + 1) * P], start=True, stop=True).then_inc(s_sc, 1)
                    pe.wait_ge(s_vw, b + 1)
                    pe.wait_ge(s_ve2, b + 1)
                    if b >= 1:
                        pe.wait_ge(s_st, b)
                    pe.matmul(bank[6][:, 0:NH * DA], kt[:, b % 2, :],
                              vw[:, b % 2, :, :].rearrange("p h d -> p (h d)"), start=True, stop=True).then_inc(s_stp, 1)
                    if b + 1 < b1_:
                        project(b + 1)
                    if b >= 1:
                        pe.wait_ge(s_oe, b)
                    n = NH * DA
                    for k in range(2):
                        pe.wait_ge(s_cm, 2 * b + k + 1)
                        for h in range(NH):
                            pe.matmul(bank[7][:, k * n + h * DA:k * n + (h + 1) * DA], cm[:, b % 2, k, h, :],
                                      va[:, b % 2, k, h, :], start=True, stop=True)
                    pe.wait_ge(s_st, b + 1)
                    pe.matmul(bank[7][:, 2 * n:3 * n], q1[:, b % 2, :],
                              st[:, b % 2, :, :].rearrange("p h d -> p (h d)"), start=True, stop=True).then_inc(s_o, 1)

            pe.wait_ge(s_tm, 1)
            attention(0, BA)

            def rowsT(j):
                if j % CH == 0:
                    pe.wait_ge(s_xs[j // CH % NX], 16 * (j // CH // NX + 1))
                if j >= 1:
                    pe.wait_ge(s_xse, j)
                pe.transpose(bank[4][:, 0:P], xs_sb[:, j // CH % NX, j % CH, :], ident[:, :]).then_inc(s_xsp, 1)

            def hidden(j, e1):
                pe.wait_ge(s_xse, j + 1)
                if j >= 2:
                    pe.wait_ge(s_uu, j - 1)
                for k in range(2):
                    hb = bank[2 * (j % 2) + k][:, :]
                    pe.matmul(hb, bhot_x[:, j, :], b_parts[:, k * HID:(k + 1) * HID], start=True, stop=False)
                    last = pe.matmul(hb, xsT[:, j % 2, :], w1_sb[:, bass.ds(e1 + k * HID, HID)], start=False, stop=True)
                last.then_inc(s_h, 1)

            def productT(j):
                pe.wait_ge(s_uu, j + 1)
                if j >= 1:
                    pe.wait_ge(s_ute, j)
                for c in range(HC):
                    last = pe.transpose(bank[5][:, c * P:(c + 1) * P], uu[:, j % 2, c * P:(c + 1) * P], ident[:, :])
                last.then_inc(s_utp, 1)

            def down(j, e2):
                pe.wait_ge(s_ute, j + 1)
                if j >= 1:
                    pe.wait_ge(s_ye, j)
                yb = bank[6][:, 0:D]
                pe.matmul(yb, bhot_x[:, j, :], b_parts[:, H2:H2 + D], start=True, stop=False)
                for c in range(HC):
                    last = pe.matmul(yb, uT[:, j % 2, c, :], w2_sb[:, bass.ds(e2 + c * D, D)],
                                     start=False, stop=(c == HC - 1))
                last.then_inc(s_yp, 1)

            pe.wait_ge(s_w1, 16 * E)
            pe.wait_ge(s_w2, 16)
            pe.wait_ge(s_bp, 7)
            pe.wait_ge(s_bexp, 1)
            experts = []
            rowsT(0)
            for j in range(NBLK + 2):
                if j + 1 < NBLK:
                    rowsT(j + 1)
                if j < NBLK:
                    e = pe.value_load(bexp_i[0:1, j:j + 1], min_val=0, max_val=E - 1)
                    hidden(j, e * H2)
                if 1 <= j <= NBLK:
                    productT(j - 1)
                if j >= 2:
                    e = pe.value_load(bexp_i[0:1, j - 2:j - 1], min_val=0, max_val=E - 1)
                    down(j - 2, e * (HC * D))

            attention(BA, B)


_INS = ["L0_attn_x", "L0_attn_wq", "L0_attn_wk", "L0_attn_wv", "L0_attn_wi", "L0_attn_bi", "L0_attn_wf", "L0_attn_bf",
        "L0_attn_ln_w", "L0_ffn_router_w", "L0_ffn_router_b", "L0_ffn_w1", "L0_ffn_b1", "L0_ffn_w2", "L0_ffn_b2"]


def kernel(**inputs):
    import numpy as _np
    import concourse.bacc as _bacc
    from concourse import mybir as _mybir
    from concourse.bass_utils import run_bass_kernel_spmd as _run

    nc = _bacc.Bacc("TRN2", target_bir_lowering=False, num_devices=1)
    arrays, args = {}, []
    for name in _INS:
        a = _np.ascontiguousarray(inputs[name])
        arrays[f"in_{name}"] = a
        args.append(nc.dram_tensor(f"in_{name}", a.shape, _mybir.dt.from_np(a.dtype), kind="ExternalInput").ap())
    shape = tuple(inputs["L0_attn_x"].shape)
    out = nc.dram_tensor("out_x", shape, _mybir.dt.float32, kind="ExternalOutput").ap()
    mlstm_moe_block(nc, *args, out)
    r = _run(nc, [arrays], core_ids=[0])
    return r.results[0]["out_x"]
```

```python
from contextlib import ExitStack

import concourse.bass as bass
from concourse import mybir

F32 = mybir.dt.float32
F32R = mybir.dt.float32r
BF16 = mybir.dt.bfloat16
I32 = mybir.dt.int32
ALU = mybir.AluOpType
ACT = mybir.ActivationFunctionType
AX = mybir.AxisListType

P = 128


def mlstm_moe_block(nc, x, wq, wk, wv, wi, bi, wf, bf, ln_w, router_w, router_b, w1, b1, w2, b2, out):
    B, S, D = x.shape
    NTOK = B * S
    T = NTOK // P
    NH = bi.shape[0]
    DH = D // NH
    DA = DH + 1
    E = w1.shape[0]
    H2 = w1.shape[2]
    HID = H2 // 2
    HC = HID // P
    R = B * NH
    NBLK = T + E - 1
    WB = H2 + H2 // P
    NX = 4
    CH = 3
    DW = D + 1
    assert NBLK % CH == 0 and S == 2 * P and D == P and R == 64
    NCH = NBLK // CH
    XG = 4
    TG = T // XG
    LG = 2
    TL = T // LG
    BA = 14
    GROUPS = [(0, 4), (4, 4), (8, 3), (11, 3), (14, 2)]
    NG = len(GROUPS)
    GT = 8
    EPS_LN = 1e-5
    EPS_N = 1e-8
    GW = R - NH
    BIG = 3.0e38

    xs_dram = nc.dram_tensor("xs_sorted", (NBLK * P, DW), F32).ap()
    y_dram = nc.dram_tensor("y_tokens", (NTOK, D), F32).ap()
    x_t = x.rearrange("b (k p) d -> p (b k) d", p=P)
    y_t = y_dram.rearrange("(t p) d -> p t d", p=P)
    out_t = out.rearrange("b (k p) d -> p (b k) d", p=P)

    ctx = ExitStack()
    with ctx:
        def sb(name, shape, dt=F32):
            return ctx.enter_context(nc.sbuf_tensor(name, shape, dt))

        def sem(name):
            return ctx.enter_context(nc.semaphore(name))

        x_sb = sb("x_sb", [P, T, D])
        xw = sb("xw", [P, T, DW])
        xn = xw[:, :, 0:D]
        yg = xn
        xnT = sb("xnT", [P, NTOK])
        u_all = sb("u_all", [P, T, NH, DA])
        w1_sb = sb("w1_sb", [P, E, WB])
        wc = sb("wc", [P, 2, WB])
        w2_sb = sb("w2_sb", [P, E * HC * D])
        xs_sb = sb("xs_sb", [P, NX, CH, DW])
        ys_sb = sb("ys_sb", [P, 2, CH, D])
        sy = sb("sy", [P, 2, D])
        pad_row = sb("pad_row", [P, DW])
        ident = sb("ident", [P, P])
        tril = sb("tril", [P, P], BF16)
        ones_bf = sb("ones_bf", [P, P], BF16)
        onesrow = sb("onesrow", [1, S])
        zeros = sb("zeros", [P, S])
        block4 = sb("block4", [P, P])
        head_mask = sb("head_mask", [P, NH, DA])
        pick_f = sb("pick_f", [P, R])
        pick = sb("pick", [P, R], F32R)
        desc8 = sb("desc8", [P, E])
        blk_start = sb("blk_start", [P, NBLK])
        nat = sb("nat", [P, 3, 4])
        natbd = sb("natbd", [P, 3, P])
        wbd = sb("wbd", [P, 3, P])
        vmean = sb("vmean", [P, NH])
        wvk = sb("wvk", [P, 2, P])
        gates_raw = sb("gates_raw", [2 * NH, 3 * D])
        gates_w = sb("gates_w", [2 * NH, D])
        gate_cols = sb("gate_cols", [P, GW + P])
        gate_bias = sb("gate_bias", [1, 2 * R])
        rw_sb = sb("rw_sb", [P, E])
        rb_sb = sb("rb_sb", [P, E])
        gamma = sb("gamma", [P, D])
        b1_nat = sb("b1_nat", [E * H2 // P, P])
        b_parts = sb("b_parts", [P, E * D], BF16)
        stats = sb("stats", [P, T, 6])
        mv = sb("mv", [P, T, 2])
        NR = 64
        veps = sb("veps", [P, NR])
        ra = sb("ra", [P, NR])
        rb_ = sb("rb_", [P, NR])
        ry = sb("ry", [P, NR])
        ry2 = sb("ry2", [P, NR])
        rstd = sb("rstd", [P, T])
        nmr = sb("nmr", [P, T])
        lg = sb("lg", [P, T, E])
        r1 = sb("r1", [P, T, E])
        rmax = sb("rmax", [P, T])
        oh = sb("oh", [P, E, T], BF16)
        cnt = sb("cnt", [P, E, T])
        csum = sb("csum", [P, E, T])
        pos3 = sb("pos3", [P, E, T])
        ecount = sb("ecount", [P, E])
        ecount_i = sb("ecount_i", [P, E], I32)
        epad_i = sb("epad_i", [P, E], I32)
        epad = sb("epad", [P, E])
        eend = sb("eend", [P, E])
        edelta = sb("edelta", [P, E])
        posf = sb("posf", [P, T])
        pos = sb("pos", [P, T], I32)
        bcmp = sb("bcmp", [P, NBLK, E])
        bexp = sb("bexp", [P, NBLK])
        bexp_i = sb("bexp_i", [P, NBLK], I32)
        ig = sb("ig", [R, S])
        fg = sb("fg", [R, S])
        ga = sb("ga", [R, S])
        gb = sb("gb", [R, S])
        gc = sb("gc", [R, S])
        lf = sb("lf", [R, S])
        fsum = sb("fsum", [R, S])
        gg = sb("gg", [R, S])
        mm = sb("mm", [R, S])
        nm = sb("nm", [R, S])
        nm2 = sb("nm2", [P, S], F32R)
        eo_row = sb("eo_row", [R, P])
        w_row = sb("w_row", [R, P])
        fl_row = sb("fl_row", [R, S])
        tm = sb("tm", [P, 6, R])
        qm = sb("qm", [P, 2, NH, S])
        q1 = sb("q1", [P, 2, P])
        kT = sb("kT", [P, 2, S])
        va = sb("va", [P, 2, 2, NH, DA])
        vw = sb("vw", [P, 2, NH, DA])
        kt = sb("kt", [P, 2, P])
        dm = sb("dm", [P, 2, 2, NH, P])
        cm = sb("cm", [P, 2, 2, NH, P])
        st = sb("st", [P, 2, NH, DA])
        ot = sb("ot", [P, NH, DA])
        sq = cm[:, 1, :, :, :].rearrange("p k h s -> p (k h s)").rearrange("p (t h d) -> p t h d", t=GT, h=NH)
        ssum = sb("ssum", [P, GT * NH])
        den = sb("den", [P, GT * NH])
        rden = sb("rden", [P, GT * NH])
        coef = sb("coef", [P, GT * NH])
        xsT = sb("xsT", [P, 2, P])
        sg = dm[:, 0, :, :, :]
        uT = dm[:, 1, :, :, :]
        b_f = dm[0:1, :, :, :, :].rearrange("p a k h s -> p (a k h s)")[:, 0:E * D]
        b_r = cm[0:1, :, :, :, :].rearrange("p a k h s -> p (a k h s)")[:, 0:E * D]

        bank = [ctx.enter_context(nc.psum_tensor(f"bank{i}", [P, 512], F32)) for i in range(8)]

        s_x = [sem(f"s_x{i}") for i in range(XG)]
        s_small = sem("s_small")
        s_const = sem("s_const")
        s_bp = sem("s_bp")
        s_xna = sem("s_xna")
        s_rs = sem("s_rs")
        s_ig = sem("s_ig")
        s_zero = sem("s_zero")
        s_fill = sem("s_fill")
        s_w1 = sem("s_w1")
        s_w2 = sem("s_w2")
        s_chain = sem("s_chain")
        s_nat = sem("s_nat")
        s_wT = sem("s_wT")
        s_wbd = sem("s_wbd")
        s_gw = sem("s_gw")
        s_xn = sem("s_xn")
        s_xT = sem("s_xT")
        s_xTe = sem("s_xTe")
        s_lg = sem("s_lg")
        s_gp = sem("s_gp")
        s_oh = sem("s_oh")
        s_cnt = sem("s_cnt")
        s_pos = sem("s_pos")
        s_scat = sem("s_scat")
        s_bexp = sem("s_bexp")
        s_b1 = sem("s_b1")
        s_wc = sem("s_wc")
        s_wv = sem("s_wv")
        s_hg = sem("s_hg")
        s_abs = sem("s_abs")
        s_u = sem("s_u")
        s_w = sem("s_w")
        s_ln = sem("s_ln")
        s_mm = sem("s_mm")
        s_rows = sem("s_rows")
        s_tmp = sem("s_tmp")
        s_tm = sem("s_tm")
        s_qkp = sem("s_qkp")
        s_qke = sem("s_qke")
        s_vp = sem("s_vp")
        s_ve = sem("s_ve")
        s_ve2 = sem("s_ve2")
        s_vw = sem("s_vw")
        s_mb = sem("s_mb")
        s_dm = sem("s_dm")
        s_dsel = sem("s_dsel")
        s_sc = sem("s_sc")
        s_cm = sem("s_cm")
        s_stp = sem("s_stp")
        s_st = sem("s_st")
        s_o = sem("s_o")
        s_oe = sem("s_oe")
        s_ones = sem("s_ones")
        s_xs = [sem(f"s_xs{i}") for i in range(NX)]
        s_xsp = sem("s_xsp")
        s_xse = sem("s_xse")
        s_h = sem("s_h")
        s_th = sem("s_th")
        s_uu = sem("s_uu")
        s_yp = sem("s_yp")
        s_ye = sem("s_ye")
        s_yst = [sem(f"s_yst{i}") for i in range(NX)]
        s_yg = [sem(f"s_yg{i}") for i in range(NG)]
        s_norm = sem("s_norm")
        s_sy = sem("s_sy")
        s_id = sem("s_id")
        s_fin = sem("s_fin")
        s_out = sem("s_out")

        NSMALL = 12
        block = ctx.enter_context(nc.Block())

        @block.sync
        def _(sp):
            for i in range(XG):
                sp.dma_start(x_sb[:, i * TG:(i + 1) * TG, :], x_t[:, i * TG:(i + 1) * TG, :]).then_inc(s_x[i], 16)
            for e in range(E):
                sp.dma_start(w1_sb[:, e, 0:H2], w1[e]).then_inc(s_w1, 16)
            sp.dma_start(w2_sb[:, :].rearrange("p (e c d) -> p e c d", e=E, c=HC),
                         w2.rearrange("e (c p) d -> p e c d", p=P)).then_inc(s_w2, 16)
            sp.wait_ge(s_id, 3)
            sp.dma_start(xs_dram.rearrange("(n p) d -> p n d", p=P),
                         pad_row[:, :].unsqueeze(1).to_broadcast([P, NBLK, DW])).then_inc(s_fill, 16)

            sp.wait_ge(s_scat, 16 * T)
            for c in range(NCH):
                if c >= NX:
                    sp.wait_ge(s_xsp, (c - NX + 1) * CH)
                    sp.wait_ge(s_yst[c % NX], 16 * CH * (c // NX))
                sp.dma_start(xs_sb[:, c % NX, :, :],
                             xs_dram[c * CH * P:(c + 1) * CH * P, :].rearrange("(n p) d -> p n d", p=P)).then_inc(s_xs[c % NX], 16)
            for i in range(NX):
                sp.wait_ge(s_yst[i], 16 * CH * len(range(i, NCH, NX)))
            for g, (b0, nb) in enumerate(GROUPS):
                ts = slice(2 * b0, 2 * (b0 + nb))
                sp.dma_start(yg[:, ts, :], y_t[:, ts, :]).then_inc(s_yg[g], 16)
            for g, (b0, nb) in enumerate(GROUPS):
                ts = slice(2 * b0, 2 * (b0 + nb))
                sp.wait_ge(s_fin, g + 1)
                sp.dma_start(out_t[:, ts, :], yg[:, ts, :]).then_inc(s_out, 16)
            sp.wait_ge(s_out, 16 * NG)

        @block.gpsimd
        def _(pool):
            pool.memset(zeros[:, :], 0.0).then_inc(s_zero, 1)
            pool.memset(pad_row[:, 0:D], 0.0).then_inc(s_id, 1)
            pool.iota(pad_row[:, D:DW].bitcast(I32), [[0, 1]], base=NTOK, channel_multiplier=1).then_inc(s_id, 1)
            pool.iota(xw[:, :, D:DW].bitcast(I32), [[P, T], [0, 1]], base=0, channel_multiplier=1).then_inc(s_id, 1)
            pool.memset(ident[:, :], 0.0).then_inc(s_const, 1)
            pool.memset(block4[:, :], 1.0).then_inc(s_const, 1)
            pool.memset(head_mask[:, :, :], 1.0).then_inc(s_const, 1)
            pool.memset(pick_f[:, :], 0.0).then_inc(s_const, 1)
            pool.memset(tril[:, :], 1.0).then_inc(s_const, 1)
            pool.wait_ge(s_const, 5)
            pool.affine_select(out=ident[:, :], in_=ident[:, :], compare_op=ALU.not_equal, fill=1.0,
                               base=0, pattern=[[-1, P]], channel_multiplier=1).then_inc(s_const, 1)
            b4 = block4[:, :].rearrange("p (g o) -> p g o", o=4)
            pool.affine_select(out=b4, in_=b4, compare_op=ALU.is_ge, fill=0.0,
                               base=0, pattern=[[-4, P // 4], [0, 4]], channel_multiplier=1).then_inc(s_const, 1)
            pool.affine_select(out=head_mask[:, :, :], in_=head_mask[:, :, :], compare_op=ALU.is_ge, fill=0.0,
                               base=0, pattern=[[-DH, NH], [0, DA]], channel_multiplier=1).then_inc(s_const, 1)
            pool.affine_select(out=pick_f[:, :], in_=pick_f[:, :], compare_op=ALU.not_equal, fill=1.0,
                               base=0, pattern=[[-1, R]], channel_multiplier=1).then_inc(s_const, 1)
            pool.affine_select(out=tril[:, :], in_=tril[:, :], compare_op=ALU.is_ge, fill=0.0,
                               base=-1, pattern=[[1, P]], channel_multiplier=-1).then_inc(s_const, 1)
            pool.wait_ge(s_const, 10)
            pool.affine_select(out=b4, in_=b4, compare_op=ALU.is_ge, fill=0.0,
                               base=3, pattern=[[4, P // 4], [0, 4]], channel_multiplier=-1).then_inc(s_const, 1)
            pool.affine_select(out=head_mask[:, :, :], in_=head_mask[:, :, :], compare_op=ALU.is_ge, fill=0.0,
                               base=DH - 1, pattern=[[DH, NH], [0, DA]], channel_multiplier=-1).then_inc(s_const, 1)
            pool.affine_select(out=pick_f[:, :], in_=pick_f[:, :], compare_op=ALU.not_equal, fill=1.0,
                               base=-R, pattern=[[-1, R]], channel_multiplier=1).then_inc(s_const, 1)
            pool.memset(ones_bf[:, :], 1.0).then_inc(s_const, 1)
            pool.memset(onesrow[:, :], 1.0).then_inc(s_const, 1)
            pool.iota(desc8[:, :], [[-1, E]], base=E, channel_multiplier=0,
                      allow_small_or_imprecise_dtypes=True).then_inc(s_const, 1)
            pool.iota(blk_start[:, :], [[P, NBLK]], base=0, channel_multiplier=0,
                      allow_small_or_imprecise_dtypes=True).then_inc(s_const, 1)
            pool.memset(va[:, :, :, :, DH:DA], 1.0).then_inc(s_ones, 1)
            pool.memset(qm[:, :, :, :], 0.0).then_inc(s_ones, 1)

            pool.wait_ge(s_small, 16 * NSMALL)
            pool.memset(b_parts[:, :], 0.0).then_inc(s_bp, 1)
            pool.wait_ge(s_bp, 1)
            pool.tensor_copy(b_parts[0:1, :], b_f).then_inc(s_bp, 1)
            pool.wait_ge(s_bp, 2)
            pool.tensor_tensor(b_r, b_f, b_parts[0:1, :], ALU.subtract).then_inc(s_bp, 1)
            pool.wait_ge(s_bp, 3)
            pool.tensor_copy(b_parts[32:33, :], b_r).then_inc(s_bp, 1)
            pool.wait_ge(s_bp, 4)
            pool.tensor_copy(b_f, b_parts[32:33, :]).then_inc(s_bp, 1)
            pool.wait_ge(s_bp, 5)
            pool.tensor_tensor(b_r, b_r, b_f, ALU.subtract).then_inc(s_bp, 1)
            pool.wait_ge(s_bp, 6)
            pool.tensor_copy(b_parts[64:65, :], b_r).then_inc(s_bp, 1)
            pool.wait_ge(s_bp, 7)

            def batch_masks(b):
                pool.wait_ge(s_ve, b + 1)
                pool.wait_ge(s_tm, 1)
                if b >= 2:
                    pool.wait_ge(s_stp, b - 1)
                pool.tensor_tensor(vw[:, b % 2, :, :], va[:, b % 2, 0, :, :],
                                   tm[:, 3, NH * b:NH * (b + 1)].unsqueeze(2).to_broadcast([P, NH, DA]),
                                   ALU.mult).then_inc(s_vw, 1)
                for k in range(2):
                    pool.wait_ge(s_dm, 2 * b + k + 1)
                    d = dm[:, b % 2, k, :, :]
                    pool.affine_select(out=d, in_=d, compare_op=ALU.is_ge, fill=0.0, base=0,
                                       pattern=[[0, NH], [1, P]], channel_multiplier=-1).then_inc(s_dsel, 1)

            for b in range(BA):
                batch_masks(b)
                if b == 1:
                    pool.wait_ge(s_fill, 16)
                    pool.wait_ge(s_pos, 1)
                if b >= 1:
                    for t in range((b - 1) * T // (BA - 1), b * T // (BA - 1)):
                        pool.indirect_dma_start(xs_dram, bass.IndirectOffsetOnAxis(ap=pos[:, t:t + 1], axis=0),
                                                xw[:, t, :], None).then_inc(s_scat, 16)
            for j in range(NBLK):
                pool.wait_ge(s_ye, j + 1)
                pool.indirect_dma_start(y_dram, bass.IndirectOffsetOnAxis(
                    ap=xs_sb[:, j // CH % NX, j % CH, D:DW].bitcast(I32), axis=0),
                    ys_sb[:, j // CH % 2, j % CH, :], None, bounds_check=NTOK - 1, oob_is_err=False).then_inc(s_yst[j // CH % NX], 16)
            for b in range(BA, B):
                batch_masks(b)

        @block.scalar
        def _(act):
            for n, w in enumerate((wq, wk, wv)):
                act.dma_start(nat[:, n, :], w.rearrange("h o i -> (h o) i")).then_inc(s_small, 16)
            act.dma_start(rw_sb[:, :], router_w).then_inc(s_small, 16)
            act.dma_start(gates_raw[0:NH, :], wi).then_inc(s_small, 16)
            act.dma_start(gates_raw[NH:2 * NH, :], wf).then_inc(s_small, 16)
            for n, v in enumerate((bf, bi)):
                act.dma_start(gate_bias[0:1, n * R:(n + 1) * R].rearrange("p (b h) -> p b h", h=NH),
                              v.partition_broadcast(B).unsqueeze(0)).then_inc(s_small, 16)
            act.dma_start(rb_sb[:, :], router_b.partition_broadcast(P)).then_inc(s_small, 16)
            act.dma_start(gamma[:, :], ln_w.partition_broadcast(P)).then_inc(s_small, 16)
            act.dma_start(b1_nat[:, :], b1.rearrange("e (c p) -> (e c) p", p=P)).then_inc(s_small, 16)
            act.dma_start(b_f, b2.rearrange("e d -> (e d)").unsqueeze(0)).then_inc(s_small, 16)
            for g in range(LG):
                act.wait_ge(s_rs, g + 1)
                for t in range(g * TL + 1, (g + 1) * TL, 2):
                    act.activation(xn[:, t, :], x_sb[:, t, :], ACT.Identity, scale=rstd[:, t:t + 1],
                                   bias=nmr[:, t:t + 1]).then_inc(s_xna, 1)
                    if t % 4 == 3 and t // 4 >= 1:
                        q = t // 4 - 1
                        act.wait_ge(s_xT, q + 1)
                        act.activation(xnT[:, q * 512:(q + 1) * 512], bank[q % 2][:, :], ACT.Copy).then_inc(s_xTe, 1)
            q = T // 4 - 1
            act.wait_ge(s_xT, q + 1)
            act.activation(xnT[:, q * 512:(q + 1) * 512], bank[q % 2][:, :], ACT.Copy).then_inc(s_xTe, 1)
            act.wait_ge(s_gp, 1)
            act.activation(ga[:, :], bank[6][0:R, 0:S], ACT.Abs).then_inc(s_abs, 1)
            act.wait_ge(s_abs, 1)
            act.activation(gb[:, :], ga[:, :], ACT.Exp, scale=-1.0).then_inc(s_u, 1)
            act.activation(ig[:, :], bank[6][R:2 * R, 0:S], ACT.Copy).then_inc(s_ig, 1)
            act.wait_ge(s_w, 1)
            act.activation(lf[:, :], gc[:, :], ACT.Ln).then_inc(s_ln, 1)
            act.wait_ge(s_mm, 2)
            act.activation(w_row[:, :], gg[:, 0:P], ACT.Exp, bias=nm[:, P - 1:P]).then_inc(s_rows, 1)
            act.activation(eo_row[:, :], mm[:, P:S], ACT.Exp, scale=-1.0, bias=mm[:, P - 1:P]).then_inc(s_rows, 1)
            act.activation(fl_row[:, :], ga[:, :], ACT.Exp, scale=-1.0).then_inc(s_rows, 1)
            def evac_qk(b):
                act.wait_ge(s_qkp, b + 1)
                if b >= 2:
                    act.wait_ge(s_o, b - 1)
                act.activation(kT[:, b % 2, :], bank[0][:, S:2 * S], ACT.Copy)
                for h in range(NH):
                    hs = slice(h * DH, (h + 1) * DH)
                    act.activation(qm[hs, b % 2, h, :], bank[0][hs, 0:S], ACT.Copy)
                act.activation(q1[:, b % 2, :], bank[0][:, P:S], ACT.Copy).then_inc(s_qke, 1)

            def decay(b):
                act.wait_ge(s_mb, b + 1)
                act.wait_ge(s_tm, 1)
                if b >= 2:
                    act.wait_ge(s_cm, 2 * (b - 1))
                for k in range(2):
                    for h in range(NH):
                        src = bank[2 + h // 2][:, (h % 2) * S + k * P:(h % 2) * S + (k + 1) * P]
                        last = act.activation(dm[:, b % 2, k, h, :], src, ACT.Exp,
                                              bias=tm[:, k, NH * b + h:NH * b + h + 1])
                    last.then_inc(s_dm, 1)

            def attention(b0, b1_):
                evac_qk(b0)
                decay(b0)
                for b in range(b0, b1_):
                    if b + 1 < b1_:
                        evac_qk(b + 1)
                        decay(b + 1)

            act.wait_ge(s_ones, 2)
            act.wait_ge(s_bp, 7)
            attention(0, BA)
            def copy_w(j):
                e = act.value_load(bexp_i[0:1, j:j + 1], min_val=0, max_val=E - 1)
                if j >= 2:
                    act.wait_ge(s_uu, j - 1)
                act.activation(wc[:, j % 2, HID:WB], w1_sb[:, bass.ds(e, 1), HID:WB], ACT.Copy).then_inc(s_wc, 1)

            act.wait_ge(s_w1, 16 * E)
            act.wait_ge(s_b1, 1)
            act.wait_ge(s_bexp, 1)
            copy_w(0)
            for j in range(NBLK + 1):
                if j < NBLK:
                    act.wait_ge(s_hg, j + 1)
                    act.wait_ge(s_wc, j + 1)
                    if j >= 2:
                        act.wait_ge(s_uu, j - 1)
                    for c in range(HC):
                        last = act.activation(sg[:, j % 2, c, :], bank[2 * (j % 2) + 1][:, c * P:(c + 1) * P], ACT.Sigmoid,
                                              bias=wc[:, j % 2, H2 + HC + c:H2 + HC + c + 1])
                    last.then_inc(s_th, 1)
                    if j + 1 < NBLK:
                        copy_w(j + 1)
                if j >= 1:
                    act.wait_ge(s_yp, j)
                    if j >= 3:
                        act.wait_ge(s_ye, j - 2)
                    act.activation(sy[:, (j - 1) % 2, :], bank[6 + (j - 1) % 2][:, 0:D], ACT.Sigmoid).then_inc(s_sy, 1)

            attention(BA, B)

        @block.vector
        def _(dve):
            chain = [0]

            def link(ins):
                chain[0] += 1
                ins.then_inc(s_chain, 1)
                dve.wait_ge(s_chain, chain[0])

            def rsqrt(v, n):
                a, b, y, y2 = ra[:, 0:n], rb_[:, 0:n], ry[:, 0:n], ry2[:, 0:n]
                link(dve.tensor_scalar(a.bitcast(I32), v.bitcast(I32), 1, None, ALU.logical_shift_right))
                link(dve.tensor_scalar(y.bitcast(I32), a.bitcast(I32), -1.0, float(0x5F3759DF), ALU.mult, ALU.add))
                for _ in range(3):
                    link(dve.tensor_tensor(a, y, y, ALU.mult))
                    link(dve.scalar_tensor_tensor(b, a, -0.5, v, ALU.mult, ALU.mult))
                    link(dve.scalar_tensor_tensor(y2, b, 1.5, y, ALU.add, ALU.mult))
                    y, y2 = y2, y
                return y

            for g in range(LG):
                for t in range(g * TL, (g + 1) * TL):
                    if t % TG == 0:
                        dve.wait_ge(s_x[t // TG], 16)
                    last = dve.bn_stats(stats[:, t, :], x_sb[:, t, :])
                link(last)
                for t in range(g * TL, (g + 1) * TL):
                    last = dve.bn_aggr(mv[:, t, :], stats[:, t, :])
                link(last)
                gs = slice(g * TL, (g + 1) * TL)
                link(dve.tensor_scalar(veps[:, 0:TL], mv[:, gs, 1], EPS_LN, None, ALU.add))
                y = rsqrt(veps[:, 0:TL], TL)
                link(dve.tensor_copy(rstd[:, gs], y))
                dve.scalar_tensor_tensor(nmr[:, gs], mv[:, gs, 0], -1.0, rstd[:, gs], ALU.mult, ALU.mult).then_inc(s_rs, 1)
                dve.wait_ge(s_rs, g + 1)
                for t in range(g * TL, (g + 1) * TL, 2):
                    dve.tensor_scalar(xn[:, t, :], x_sb[:, t, :], rstd[:, t:t + 1], nmr[:, t:t + 1],
                                      ALU.mult, ALU.add).then_inc(s_xn, 1)
                if g == 0:
                    dve.wait_ge(s_small, 16 * NSMALL)
                    dve.wait_ge(s_const, 17)
                    for n in range(3):
                        dve.tensor_tensor(natbd[:, n, :].rearrange("p (g i) -> p g i", i=4),
                                          block4[:, :].rearrange("p (g i) -> p g i", i=4),
                                          nat[:, n, :].unsqueeze(1).to_broadcast([P, P // 4, 4]),
                                          ALU.mult).then_inc(s_nat, 1)
                    link(dve.tensor_tensor(gates_w[:, :], gates_raw[:, 0:D], gates_raw[:, D:2 * D], ALU.add))
                    dve.tensor_tensor(gates_raw[:, 0:D], gates_w[:, :], gates_raw[:, 2 * D:3 * D], ALU.add).then_inc(s_nat, 1)
                    dve.memset(gate_cols[:, :], 0.0).then_inc(s_chain, 1)
                    chain[0] += 1
                    dve.tensor_copy(pick[:, :], pick_f[:, :]).then_inc(s_nat, 1)
                    dve.tensor_scalar(gamma[:, :], gamma[:, :], 1.0, None, ALU.add).then_inc(s_chain, 1)
                    chain[0] += 1
                    dve.wait_ge(s_wT, 1)
                    link(dve.tensor_copy(wbd[:, :, :], bank[4][:, 0:3 * P].rearrange("p (n m) -> p n m", n=3)))
                    dve.tensor_copy(w1_sb[:, :, H2:WB], bank[5][:, 0:E * (WB - H2)].rearrange("p (e c) -> p e c", e=E)).then_inc(s_b1, 1)
                    link(dve.tensor_copy(gate_cols[:, GW + R:GW + R + NH], bank[4][:, 3 * P:3 * P + NH]))
                    link(dve.tensor_copy(gate_cols[:, GW:GW + NH], bank[4][:, 3 * P + NH:3 * P + 2 * NH]))
                    link(dve.tensor_scalar(wvk[:, 1, :], wbd[:, 1, :], float(DH) ** -0.5, None, ALU.mult))
                    link(dve.tensor_reduce(vmean[:, :], wbd[:, 2, :].rearrange("p (h d) -> p h d", h=NH), AX.X, ALU.add))
                    link(dve.tensor_scalar(vmean[:, :], vmean[:, :], -1.0 / DH, None, ALU.mult))
                    dve.tensor_tensor(wvk[:, 0, :].rearrange("p (h d) -> p h d", h=NH),
                                      wbd[:, 2, :].rearrange("p (h d) -> p h d", h=NH),
                                      vmean[:, :].unsqueeze(2).to_broadcast([P, NH, DH]), ALU.add).then_inc(s_wbd, 1)

            dve.wait_ge(s_lg, 1)
            link(dve.tensor_tensor(lg[:, :, :], bank[2][:, 0:T * E].rearrange("p (t e) -> p t e", e=E),
                                   rb_sb[:, :].unsqueeze(1).to_broadcast([P, T, E]), ALU.add))
            link(dve.tensor_reduce(rmax[:, :], lg[:, :, :], AX.X, ALU.max))
            link(dve.tensor_tensor(r1[:, :, :], lg[:, :, :], rmax[:, :].unsqueeze(2).to_broadcast([P, T, E]), ALU.is_equal))
            link(dve.tensor_tensor(lg[:, :, :], r1[:, :, :], desc8[:, :].unsqueeze(1).to_broadcast([P, T, E]), ALU.mult))
            link(dve.tensor_reduce(rmax[:, :], lg[:, :, :], AX.X, ALU.max))
            dve.tensor_tensor(oh[:, :, :].rearrange("p e t -> p t e"), rmax[:, :].unsqueeze(2).to_broadcast([P, T, E]),
                              desc8[:, :].unsqueeze(1).to_broadcast([P, T, E]), ALU.is_equal).then_inc(s_oh, 1)
            dve.wait_ge(s_u, 1)
            link(dve.tensor_scalar(gc[:, :], gb[:, :], 1.0, None, ALU.add))
            dve.scalar_tensor_tensor(gb[:, :], gc[:, :], -1.0, gb[:, :], ALU.add, ALU.subtract).then_inc(s_w, 1)
            dve.wait_ge(s_cnt, 1)
            link(dve.tensor_copy(cnt[:, :, :], bank[3][:, 0:E * T].rearrange("p (e t) -> p e t", e=E)))
            link(dve.tensor_copy(pos3[:, :, :], bank[3][:, E * T:2 * E * T].rearrange("p (e t) -> p e t", e=E)))
            dve.wait_ge(s_ln, 1)
            dve.wait_ge(s_w, 1)
            link(dve.tensor_tensor(gc[:, :], gb[:, :], lf[:, :], ALU.subtract))
            link(dve.scalar_tensor_tensor(lf[:, :], bank[6][0:R, 0:S], 0.0, gc[:, :], ALU.min, ALU.add))
            link(dve.tensor_tensor_scan(fsum[:, :], lf[:, :], zeros[0:R, :], 0.0, ALU.add, ALU.add))
            dve.wait_ge(s_ig, 1)
            link(dve.tensor_tensor(gg[:, :], ig[:, :], fsum[:, :], ALU.subtract))
            link(dve.tensor_tensor_scan(mm[:, :], gg[:, :], gg[:, :], -BIG, ALU.max, ALU.max))
            dve.tensor_tensor(ga[:, :], fsum[:, :], mm[:, :], ALU.add).then_inc(s_mm, 1)
            link(dve.tensor_scalar(nm[:, :], mm[:, :], -1.0, None, ALU.mult))
            link(dve.tensor_copy(nm2[0:R, :], nm[:, :]))
            dve.tensor_tensor(nm2[R:2 * R, :], nm[:, :], nm2[0:R, :].bitcast(F32), ALU.subtract).then_inc(s_mm, 1)
            dve.wait_ge(s_tmp, 1)
            dve.tensor_copy(tm[:, :, :], bank[7][:, 0:6 * R].rearrange("p (n r) -> p n r", n=6)).then_inc(s_tm, 1)
            dve.wait_ge(s_tm, 1)
            dve.wait_ge(s_ones, 2)
            dve.wait_ge(s_bp, 7)

            def routing(part):
                flat = "p e t -> p (e t)"
                if part == 0:
                    link(dve.tensor_tensor_scan(csum[:, :, :].rearrange(flat), cnt[:, :, :].rearrange(flat),
                                                zeros[:, 0:E * T], 0.0, ALU.add, ALU.add))
                    link(dve.tensor_reduce(ecount[:, :], cnt[:, :, :], AX.X, ALU.add))
                if part == 1:
                    link(dve.tensor_scalar(ecount_i[:, :], ecount[:, :], float(P - 1), None, ALU.add))
                    link(dve.tensor_scalar(epad_i[:, :], ecount_i[:, :], 7, 7, ALU.logical_shift_right, ALU.logical_shift_left))
                    link(dve.tensor_copy(epad[:, :], epad_i[:, :]))
                    link(dve.tensor_tensor_scan(eend[:, :], epad[:, :], zeros[:, 0:E], 0.0, ALU.add, ALU.add))
                    link(dve.tensor_tensor(edelta[:, :], eend[:, :], epad[:, :], ALU.subtract))
                    link(dve.tensor_tensor(edelta[:, :], edelta[:, :], csum[:, :, T - 1], ALU.subtract))
                    link(dve.tensor_tensor(edelta[:, :], edelta[:, :], ecount[:, :], ALU.add))
                    link(dve.tensor_tensor(csum[:, :, :], csum[:, :, :], cnt[:, :, :], ALU.subtract))
                    link(dve.tensor_tensor(csum[:, :, :], csum[:, :, :], edelta[:, :].unsqueeze(2).to_broadcast([P, E, T]), ALU.add))
                    link(dve.tensor_tensor(pos3[:, :, :], pos3[:, :, :], csum[:, :, :], ALU.add))
                    link(dve.tensor_tensor(pos3[:, :, :], pos3[:, :, :], oh[:, :, :], ALU.mult))
                    link(dve.tensor_reduce(posf[:, :], pos3[:, :, :].rearrange("p e t -> p t e"), AX.X, ALU.add))
                    dve.tensor_copy(pos[:, :], posf[:, :]).then_inc(s_pos, 1)
                if part == 2:
                    link(dve.tensor_tensor(bcmp[:, :, :], blk_start[:, :].unsqueeze(2).to_broadcast([P, NBLK, E]),
                                           eend[:, :].unsqueeze(1).to_broadcast([P, NBLK, E]), ALU.is_ge))
                    link(dve.tensor_reduce(bexp[:, :], bcmp[:, :, :], AX.X, ALU.add))
                    link(dve.tensor_scalar(bexp[:, :], bexp[:, :], float(E - 1), None, ALU.min))
                    dve.tensor_copy(bexp_i[:, :], bexp[:, :]).then_inc(s_bexp, 1)
    
            def evac_v(b):
                dve.wait_ge(s_vp, b + 1)
                if b >= 2:
                    dve.wait_ge(s_o, b - 1)
                    dve.wait_ge(s_vw, b - 1)
                dve.tensor_copy(va[:, b % 2, :, :, 0:DH],
                                bank[1][:, :].rearrange("p (k h d) -> p k h d", k=2, d=DH)[:, :, 0:NH, :]).then_inc(s_ve, 1)
                dve.tensor_copy(kt[:, b % 2, :], bank[1][:, P:2 * P]).then_inc(s_ve2, 1)

            def scores(b):
                for k in range(2):
                    dve.wait_ge(s_sc, 2 * b + k + 1)
                    dve.wait_ge(s_dsel, 2 * b + k + 1)
                    if b >= 2:
                        dve.wait_ge(s_o, b - 1)
                    dve.tensor_tensor(cm[:, b % 2, k, :, :], dm[:, b % 2, k, :, :],
                                      bank[4 + k][:, :].rearrange("p (h s) -> p h s", h=NH), ALU.mult).then_inc(s_cm, 1)

            def state(b):
                dve.wait_ge(s_stp, b + 1)
                if b >= 2:
                    dve.wait_ge(s_o, b - 1)
                dve.tensor_tensor(st[:, b % 2, :, :], head_mask[:, :, :],
                                  bank[6][:, 0:NH * DA].rearrange("p (h d) -> p h d", h=NH), ALU.mult).then_inc(s_st, 1)

            def outputs(b):
                dve.wait_ge(s_o, b + 1)
                hd = "p (h d) -> p h d"
                n = NH * DA
                dve.tensor_copy(u_all[:, 2 * b, :, :], bank[7][:, 0:n].rearrange(hd, h=NH))
                link(dve.tensor_tensor(ot[:, :, :], bank[7][:, 2 * n:3 * n].rearrange(hd, h=NH),
                                       tm[:, 2, NH * b:NH * (b + 1)].unsqueeze(2).to_broadcast([P, NH, DA]), ALU.mult))
                dve.tensor_tensor(u_all[:, 2 * b + 1, :, :], ot[:, :, :], bank[7][:, n:2 * n].rearrange(hd, h=NH),
                                  ALU.add).then_inc(s_oe, 1)

            def attention(b0, b1_):
                evac_v(b0)
                for b in range(b0, b1_):
                    state(b)
                    scores(b)
                    if b + 1 < b1_:
                        evac_v(b + 1)
                    outputs(b)
                    if b in (0, 1, 2):
                        routing(b)

            def normalise(g, part):
                b0, nb = GROUPS[g]
                nt = 2 * nb
                n = nt * NH
                uv = u_all[:, 2 * b0:2 * b0 + nt, :, 0:DH]
                rs = u_all[:, 2 * b0:2 * b0 + nt, :, DH]
                dn = den[:, 0:n].rearrange("p (t h) -> p t h", h=NH)
                rd = rden[:, 0:n].rearrange("p (t h) -> p t h", h=NH)
                if part == 0:
                    dve.wait_ge(s_oe, b0 + nb)
                    link(dve.tensor_tensor(sq[:, 0:nt, :, :], uv, uv, ALU.mult))
                    link(dve.tensor_reduce(ssum[:, 0:n], sq[:, 0:nt, :, :], AX.X, ALU.add))
                if part == 1:
                    link(dve.tensor_scalar(rd, rs, -1.0, None, ALU.mult))
                    link(dve.tensor_tensor(dn, rd, rs, ALU.max))
                    fl = tm[:, 4:6, b0 * NH:(b0 + nb) * NH].rearrange("p k (b h) -> p b k h", h=NH)
                    d4 = den[:, 0:n].rearrange("p (b k h) -> p b k h", k=2, h=NH)
                    link(dve.tensor_tensor(d4, d4, fl, ALU.max))
                    link(dve.tensor_scalar(den[:, 0:n], den[:, 0:n], EPS_N, None, ALU.add))
                    link(dve.reciprocal(rden[:, 0:n], den[:, 0:n]))
                    link(dve.scalar_tensor_tensor(ssum[:, 0:n], ssum[:, 0:n], 1.0 / DH, rden[:, 0:n], ALU.mult, ALU.mult))
                    link(dve.tensor_tensor(ssum[:, 0:n], ssum[:, 0:n], rden[:, 0:n], ALU.mult))
                    link(dve.tensor_scalar(veps[:, 0:n], ssum[:, 0:n], EPS_LN, None, ALU.add))
                if part == 2:
                    y = rsqrt(veps[:, 0:n], n)
                    link(dve.scalar_tensor_tensor(coef[:, 0:n], y, 1.0, rden[:, 0:n], ALU.mult, ALU.mult))
                if part == 3:
                    link(dve.tensor_tensor(sq[:, 0:nt, :, :], uv,
                                           coef[:, 0:n].rearrange("p (t h) -> p t h", h=NH).unsqueeze(3).to_broadcast([P, nt, NH, DH]), ALU.mult))
                    link(dve.tensor_tensor(uv, sq[:, 0:nt, :, :],
                                           gamma[:, :].rearrange("p (h d) -> p h d", h=NH).unsqueeze(1).to_broadcast([P, nt, NH, DH]), ALU.mult))

            def finish(g):
                b0, nb = GROUPS[g]
                ts = slice(2 * b0, 2 * (b0 + nb))
                y = yg[:, ts, :]
                hd = "p t (h d) -> p t h d"
                dve.wait_ge(s_yg[g], 16)
                link(dve.tensor_tensor(y.rearrange(hd, h=NH), y.rearrange(hd, h=NH), u_all[:, ts, :, 0:DH], ALU.mult))
                dve.tensor_tensor(y, y, x_sb[:, ts, :], ALU.add).then_inc(s_fin, 1)

            attention(0, BA)

            def evac_xs(j):
                dve.wait_ge(s_xsp, j + 1)
                if j >= 2:
                    dve.wait_ge(s_h, j - 1)
                dve.tensor_copy(xsT[:, j % 2, :], bank[4][:, 0:P]).then_inc(s_xse, 1)

            def product(j):
                dve.wait_ge(s_th, j + 1)
                dve.wait_ge(s_h, j + 1)
                if j >= 2:
                    dve.wait_ge(s_yp, j - 1)
                for c in range(HC):
                    last = dve.scalar_tensor_tensor(uT[:, j % 2, c, :], bank[2 * (j % 2)][:, c * P:(c + 1) * P],
                                                    wc[:, j % 2, H2 + c:H2 + c + 1], sg[:, j % 2, c, :], ALU.add, ALU.mult)
                last.then_inc(s_uu, 1)

            def evac_y(j):
                dve.wait_ge(s_sy, j + 1)
                c = j // CH - 2
                if c >= 0 and j % CH == 0:
                    dve.wait_ge(s_yst[c % NX], 16 * CH * (c // NX + 1))
                dve.tensor_tensor(ys_sb[:, (j // CH) % 2, j % CH, :], sy[:, j % 2, :], bank[6 + j % 2][:, 0:D], ALU.mult).then_inc(s_ye, 1)

            def copy_w(j):
                e = dve.value_load(bexp_i[0:1, j:j + 1], min_val=0, max_val=E - 1)
                if j >= 2:
                    dve.wait_ge(s_h, j - 1)
                dve.tensor_copy(wc[:, j % 2, 0:HID], w1_sb[:, bass.ds(e, 1), 0:HID]).then_inc(s_wv, 1)

            dve.wait_ge(s_w1, 16 * E)
            dve.wait_ge(s_bexp, 1)
            evac_xs(0)
            copy_w(0)
            for j in range(NBLK + 1):
                if j + 1 < NBLK:
                    evac_xs(j + 1)
                    copy_w(j + 1)
                if j < NBLK:
                    product(j)
                if j >= 1:
                    evac_y(j - 1)
                if 4 <= j < 36 and j % 2 == 0:
                    normalise((j - 4) // 8, (j - 4) // 2 % 4)

            attention(BA, B)
            for part in range(4):
                normalise(4, part)
            for g in range(NG):
                finish(g)

        @block.tensor
        def _(pe):
            def transposes(q):
                pe.wait_ge(s_xn, 2 * (q + 1))
                pe.wait_ge(s_xna, 2 * (q + 1))
                if q >= 2:
                    pe.wait_ge(s_xTe, q - 1)
                for i in range(4):
                    last = pe.transpose(bank[q % 2][:, i * P:(i + 1) * P], xn[:, 4 * q + i, :], ident[:, :])
                last.then_inc(s_xT, 1)

            def logits(q):
                pe.wait_ge(s_xTe, q + 1)
                for t in range(4 * q, 4 * q + 4):
                    last = pe.matmul(bank[2][:, t * E:(t + 1) * E], xnT[:, t * P:(t + 1) * P], rw_sb[:, :],
                                     start=True, stop=True)
                if q == T // 4 - 1:
                    last.then_inc(s_lg, 1)

            def gates(b):
                pe.matmul(bank[6][:, 0:S], gate_cols[:, GW - NH * b:GW - NH * b + P], xnT[:, b * S:(b + 1) * S],
                          start=(b == 0), stop=False)

            pe.wait_ge(s_const, 17)
            for q in range(T // 4):
                transposes(q)
                if q == 0:
                    pe.wait_ge(s_nat, 5)
                    for n in range(3):
                        pe.transpose(bank[4][:, n * P:(n + 1) * P], natbd[:, n, :], ident[:, :])
                    pe.transpose(bank[4][:, 3 * P:3 * P + 2 * NH], gates_raw[:, 0:D], ident[0:2 * NH, 0:2 * NH])
                    pe.transpose(bank[5][:, 0:E * (WB - H2)], b1_nat[:, :], ident[0:E * (WB - H2), 0:E * (WB - H2)]).then_inc(s_wT, 1)
                if q >= 1:
                    logits(q - 1)
                if q == T // 8:
                    pe.wait_ge(s_wbd, 1)
                    for b in range(2 * q):
                        gates(b)
                elif q > T // 8:
                    gates(2 * q - 2)
                    gates(2 * q - 1)
            logits(T // 4 - 1)
            gates(B - 2)
            gates(B - 1)
            pe.matmul(bank[6][:, 0:S], gate_bias[0:1, :], onesrow[0:1, :], start=False, stop=True).then_inc(s_gp, 1)
            pe.wait_ge(s_oh, 1)
            ohf = oh[:, :, :].rearrange("p e t -> p (e t)")
            pe.matmul(bank[3][:, 0:E * T], ones_bf[:, :], ohf, start=True, stop=True)
            pe.matmul(bank[3][:, E * T:2 * E * T], tril[:, :], ohf, start=True, stop=True).then_inc(s_cnt, 1)
            pe.wait_ge(s_mm, 2)
            pe.wait_ge(s_rows, 3)
            idr = ident[0:R, 0:R]
            for n, v in enumerate((gg[:, 0:P], gg[:, P:S], eo_row[:, :], w_row[:, :], fl_row[:, 0:P], fl_row[:, P:S])):
                last = pe.transpose(bank[7][:, n * R:(n + 1) * R], v, idr)
            last.then_inc(s_tmp, 1)

            def project(b):
                xb = xnT[:, b * S:(b + 1) * S]
                if b >= 1:
                    pe.wait_ge(s_qke, b)
                pe.matmul(bank[0][:, 0:S], wbd[:, 0, :], xb, start=True, stop=True)
                pe.matmul(bank[0][:, S:2 * S], wvk[:, 1, :], xb, start=True, stop=True).then_inc(s_qkp, 1)
                if b >= 1:
                    pe.wait_ge(s_ve2, b)
                wv_k = wvk[:, :, :].rearrange("p n m -> p (n m)")
                pe.matmul(bank[1][:, 0:2 * P], xnT[:, b * S:b * S + P], wv_k, start=True, stop=True)
                pe.matmul(bank[1][:, 2 * P:3 * P], xnT[:, b * S + P:(b + 1) * S], wvk[:, 0, :], start=True, stop=True).then_inc(s_vp, 1)
                if b >= 1:
                    pe.wait_ge(s_dm, 2 * b)
                for h in range(NH):
                    r = NH * b + h
                    last = pe.matmul(bank[2 + h // 2][:, (h % 2) * S:(h % 2 + 1) * S],
                                     pick[:, r:r + 1].to_broadcast([P, P]), nm2[:, :], start=True, stop=True)
                last.then_inc(s_mb, 1)

            def attention(b0, b1_):
                project(b0)
                for b in range(b0, b1_):
                    pe.wait_ge(s_qke, b + 1)
                    if b >= 1:
                        pe.wait_ge(s_cm, 2 * b)
                    for k in range(2):
                        pe.matmul(bank[4 + k][:, :], kT[:, b % 2, k * P:(k + 1) * P],
                                  qm[:, b % 2, :, k * P:(k + 1) * P], start=True, stop=True).then_inc(s_sc, 1)
                    pe.wait_ge(s_vw, b + 1)
                    pe.wait_ge(s_ve2, b + 1)
                    if b >= 1:
                        pe.wait_ge(s_st, b)
                    pe.matmul(bank[6][:, 0:NH * DA], kt[:, b % 2, :],
                              vw[:, b % 2, :, :].rearrange("p h d -> p (h d)"), start=True, stop=True).then_inc(s_stp, 1)
                    if b + 1 < b1_:
                        project(b + 1)
                    if b >= 1:
                        pe.wait_ge(s_oe, b)
                    n = NH * DA
                    for k in range(2):
                        pe.wait_ge(s_cm, 2 * b + k + 1)
                        for h in range(NH):
                            pe.matmul(bank[7][:, k * n + h * DA:k * n + (h + 1) * DA], cm[:, b % 2, k, h, :],
                                      va[:, b % 2, k, h, :], start=True, stop=True)
                    pe.wait_ge(s_st, b + 1)
                    pe.matmul(bank[7][:, 2 * n:3 * n], q1[:, b % 2, :],
                              st[:, b % 2, :, :].rearrange("p h d -> p (h d)"), start=True, stop=True).then_inc(s_o, 1)

            pe.wait_ge(s_tm, 1)
            attention(0, BA)

            def rowsT(j):
                if j % CH == 0:
                    pe.wait_ge(s_xs[j // CH % NX], 16 * (j // CH // NX + 1))
                if j >= 1:
                    pe.wait_ge(s_xse, j)
                pe.transpose(bank[4][:, 0:P], xs_sb[:, j // CH % NX, j % CH, 0:D], ident[:, :]).then_inc(s_xsp, 1)

            def hidden(j):
                pe.wait_ge(s_xse, j + 1)
                pe.wait_ge(s_wc, j + 1)
                if j >= 2:
                    pe.wait_ge(s_uu, j - 1)
                for k, done in ((1, s_hg), (0, s_h)):
                    if k == 0:
                        pe.wait_ge(s_wv, j + 1)
                    for c in range(HC):
                        m = (k * HC + c) * P
                        last = pe.matmul(bank[2 * (j % 2) + k][:, c * P:(c + 1) * P], wc[:, j % 2, m:m + P],
                                         xsT[:, j % 2, :], start=True, stop=True)
                    last.then_inc(done, 1)

            def down(j, e):
                pe.wait_ge(s_uu, j + 1)
                if j >= 2:
                    pe.wait_ge(s_ye, j - 1)
                yb = bank[6 + j % 2][:, 0:D]
                pe.matmul(yb, ones_bf[0:65, :], b_parts[0:65, bass.ds(e * D, D)], start=True, stop=False)
                for c in range(HC):
                    last = pe.matmul(yb, uT[:, j % 2, c, :], w2_sb[:, bass.ds(e * (HC * D) + c * D, D)],
                                     start=False, stop=(c == HC - 1))
                last.then_inc(s_yp, 1)

            pe.wait_ge(s_w2, 16)
            pe.wait_ge(s_bp, 7)
            pe.wait_ge(s_bexp, 1)
            rowsT(0)
            for j in range(NBLK + 1):
                if j + 1 < NBLK:
                    rowsT(j + 1)
                if j < NBLK:
                    hidden(j)
                if j >= 1:
                    down(j - 1, pe.value_load(bexp_i[0:1, j - 1:j], min_val=0, max_val=E - 1))

            attention(BA, B)


_INS = ["L0_attn_x", "L0_attn_wq", "L0_attn_wk", "L0_attn_wv", "L0_attn_wi", "L0_attn_bi", "L0_attn_wf", "L0_attn_bf",
        "L0_attn_ln_w", "L0_ffn_router_w", "L0_ffn_router_b", "L0_ffn_w1", "L0_ffn_b1", "L0_ffn_w2", "L0_ffn_b2"]


def kernel(**inputs):
    import numpy as _np
    import concourse.bacc as _bacc
    from concourse import mybir as _mybir
    from concourse.bass_utils import run_bass_kernel_spmd as _run

    nc = _bacc.Bacc("TRN2", target_bir_lowering=False, num_devices=1)
    arrays, args = {}, []
    for name in _INS:
        a = _np.ascontiguousarray(inputs[name])
        arrays[f"in_{name}"] = a
        args.append(nc.dram_tensor(f"in_{name}", a.shape, _mybir.dt.from_np(a.dtype), kind="ExternalInput").ap())
    shape = tuple(inputs["L0_attn_x"].shape)
    out = nc.dram_tensor("out_x", shape, _mybir.dt.float32, kind="ExternalOutput").ap()
    mlstm_moe_block(nc, *args, out)
    r = _run(nc, [arrays], core_ids=[0])
    return r.results[0]["out_x"]
```

```python
from contextlib import ExitStack

import concourse.bass as bass
from concourse import mybir

F32 = mybir.dt.float32
F32R = mybir.dt.float32r
BF16 = mybir.dt.bfloat16
I32 = mybir.dt.int32
ALU = mybir.AluOpType
ACT = mybir.ActivationFunctionType
AX = mybir.AxisListType

P = 128


def mlstm_moe_block(nc, x, wq, wk, wv, wi, bi, wf, bf, ln_w, router_w, router_b, w1, b1, w2, b2, out):
    B, S, D = x.shape
    NTOK = B * S
    T = NTOK // P
    NH = bi.shape[0]
    DH = D // NH
    DA = DH + 1
    E = w1.shape[0]
    H2 = w1.shape[2]
    HID = H2 // 2
    HC = HID // P
    R = B * NH
    NBLK = T + E - 1
    WB = H2 + H2 // P
    NX = 4
    CH = 3
    DW = D + 1
    assert NBLK % CH == 0 and S == 2 * P and D == P and R == 64
    NCH = NBLK // CH
    XG = 8
    TG = T // XG
    DVE_Q = (2, 4, 6)
    GROUPS = [(0, 4), (4, 4), (8, 4), (12, 4)]
    NPC = 8
    TP = T // NPC
    POOL_PIECES = (2, 4, 6)
    PE_PIECES = (0, 1, 3, 5)
    NSTEPS = 25
    GAMMA_AT = (9, 18, 27, 34)
    GT = 8
    EPS_LN = 1e-5
    EPS_N = 1e-8
    NL = E + 2 * NH
    BIG = 3.0e38

    xs_dram = nc.dram_tensor("xs_sorted", (NBLK * P, DW), F32).ap()
    y_dram = nc.dram_tensor("y_tokens", (NTOK, D), F32).ap()
    m_dram = nc.dram_tensor("minus_max", (R, S), F32).ap()
    x_t = x.rearrange("b (k p) d -> p (b k) d", p=P)
    y_t = y_dram.rearrange("(t p) d -> p t d", p=P)
    out_t = out.rearrange("b (k p) d -> p (b k) d", p=P)

    ctx = ExitStack()
    with ctx:
        def sb(name, shape, dt=F32):
            return ctx.enter_context(nc.sbuf_tensor(name, shape, dt))

        def sem(name):
            return ctx.enter_context(nc.semaphore(name))

        x_sb = sb("x_sb", [P, T, D])
        xw = sb("xw", [P, T, DW])
        xn = xw[:, :, 0:D]
        yg = xn
        xnT = sb("xnT", [P, NTOK])
        u_all = sb("u_all", [P, T, NH, DA])
        w1_sb = sb("w1_sb", [P, E, WB])
        wc = sb("wc", [P, 3, WB])
        w2_sb = sb("w2_sb", [P, E * HC * D])
        xs_sb = sb("xs_sb", [P, NX, CH, DW])
        pad_row = sb("pad_row", [P, DW])
        ident = sb("ident", [P, P])
        tril = sb("tril", [P, P], BF16)
        ones_bf = sb("ones_bf", [P, P], BF16)
        zeros = sb("zeros", [P, S])
        block4 = sb("block4", [P, P])
        head_mask = sb("head_mask", [P, NH, DA])
        desc8 = sb("desc8", [P, E])
        blk_start = sb("blk_start", [P, NBLK])
        nat = sb("nat", [P, 3, 4])
        wqk = sb("wqk", [P, P])
        wbd = sb("wbd", [P, P])
        vmean = sb("vmean", [P, NH])
        wvc = sb("wvc", [P, P])
        gtok = sb("gtok", [P, 2, 2, B, NH])
        rw_sb = sb("rw_sb", [P, NL])
        rb_sb = sb("rb_sb", [P, NL])
        gamma = sb("gamma", [P, D])
        b1_nat = sb("b1_nat", [E * H2 // P, P])
        b2_sb = sb("b2_sb", [P, E, D])
        stats = sb("stats", [P, T, 6])
        mv = sb("mv", [P, T, 2])
        NR = 64
        veps = sb("veps", [P, NR])
        ra = sb("ra", [P, NR])
        rb_ = sb("rb_", [P, NR])
        ry = sb("ry", [P, NR])
        ry2 = sb("ry2", [P, NR])
        rstd = sb("rstd", [P, T])
        nmr = sb("nmr", [P, T])
        lg = sb("lg", [P, T, E])
        r1 = sb("r1", [P, T, E])
        rmax = sb("rmax", [P, T])
        oh = sb("oh", [P, E, T], BF16)
        cnt = sb("cnt", [P, E, T])
        csum = sb("csum", [P, E, T])
        pos3 = sb("pos3", [P, E, T])
        ecount = sb("ecount", [P, E])
        ecount_i = sb("ecount_i", [P, E], I32)
        epad_i = sb("epad_i", [P, E], I32)
        epad = sb("epad", [P, E])
        eend = sb("eend", [P, E])
        edelta = sb("edelta", [P, E])
        posf = sb("posf", [P, T])
        pos = sb("pos", [P, T], I32)
        bcmp = sb("bcmp", [P, NBLK, E])
        bexp = sb("bexp", [P, NBLK])
        bexp_i = sb("bexp_i", [P, NBLK], I32)
        mb = sb("mb", [P, 2, NH, S])
        spare = sb("spare", [P, 1])
        ig = sb("ig", [R, S])
        fg = sb("fg", [R, S])
        ga = sb("ga", [R, S])
        gb = sb("gb", [R, S])
        gc = sb("gc", [R, S])
        lf = sb("lf", [R, S])
        fsum = sb("fsum", [R, S])
        gg = sb("gg", [R, S])
        mm = sb("mm", [R, S])
        nm = sb("nm", [R, S])
        eo_row = sb("eo_row", [R, P])
        w_row = sb("w_row", [R, P])
        fl_row = sb("fl_row", [R, S])
        tm = sb("tm", [P, 6, R])
        qm = sb("qm", [P, 2, NH, S])
        q1 = sb("q1", [P, 2, P])
        va = sb("va", [P, 2, 2, NH, DA])
        vw = sb("vw", [P, 2, NH, DA])
        dm = sb("dm", [P, 2, 2, NH, P])
        cm = sb("cm", [P, 2, 2, NH, P])
        st = sb("st", [P, 2, NH, DA])
        ot = sb("ot", [P, NH, DA])
        sqs = [cm[:, i, :, :, :].rearrange("p k h s -> p (k h s)").rearrange("p (t h d) -> p t h d", t=GT, h=NH)
               for i in range(2)]
        ssum = sb("ssum", [P, GT * NH])
        den = sb("den", [P, GT * NH])
        rden = sb("rden", [P, GT * NH])
        coef = sb("coef", [P, GT * NH])
        qflat = qm[:, :, :, :].rearrange("p a h s -> p (a h s)")
        ys_sb = qflat[:, 0:2 * CH * D].rearrange("p (i n d) -> p i n d", i=2, n=CH)
        yb = qflat[:, 6 * D:8 * D].rearrange("p (i d) -> p i d", i=2)
        sy = qflat[:, 8 * D:10 * D].rearrange("p (i d) -> p i d", i=2)
        xsT = qflat[:, 10 * D:12 * D].rearrange("p (i d) -> p i d", i=2)
        sg = dm[:, 0, :, :, :]
        uT = dm[:, 1, :, :, :]
        wflat = dm[:, 1, :, :, :].rearrange("p k h s -> p (k h s)")
        natbd = wflat[:, 0:3 * P].rearrange("p (n m) -> p n m", n=3)
        gates_raw = wflat[0:2 * NH, 3 * P:3 * P + 3 * D]
        gates_w = wflat[0:2 * NH, 3 * P + 3 * D:3 * P + 4 * D]

        bank = [ctx.enter_context(nc.psum_tensor(f"bank{i}", [P, 512], F32)) for i in range(8)]

        xT_bank = [bank[i] for i in (0, 1, 3, 7)]

        s_x = [sem(f"s_x{i}") for i in range(XG)]
        s_small = sem("s_small")
        s_const = sem("s_const")
        s_yb = sem("s_yb")
        s_xna = sem("s_xna")
        s_xnp = sem("s_xnp")
        s_rs = sem("s_rs")
        s_ig = sem("s_ig")
        s_zero = sem("s_zero")
        s_fill = sem("s_fill")
        s_w1 = sem("s_w1")
        s_w2 = sem("s_w2")
        s_chain = sem("s_chain")
        s_nat = sem("s_nat")
        s_wT = sem("s_wT")
        s_wts = sem("s_wts")
        s_gw = sem("s_gw")
        s_xn = sem("s_xn")
        s_xT = sem("s_xT")
        s_xTe = sem("s_xTe")
        s_xTd = sem("s_xTd")
        s_gt = sem("s_gt")
        s_lg = sem("s_lg")
        s_gp = sem("s_gp")
        s_oh = sem("s_oh")
        s_cnt = sem("s_cnt")
        s_pos = sem("s_pos")
        s_scat = sem("s_scat")
        s_bexp = sem("s_bexp")
        s_wc = sem("s_wc")
        s_prep = sem("s_prep")
        s_wv = sem("s_wv")
        s_hg = sem("s_hg")
        s_abs = sem("s_abs")
        s_u = sem("s_u")
        s_w = sem("s_w")
        s_ln = sem("s_ln")
        s_mm = sem("s_mm")
        s_rows = sem("s_rows")
        s_tmp = sem("s_tmp")
        s_tm = sem("s_tm")
        s_qkp = sem("s_qkp")
        s_qke = sem("s_qke")
        s_vp = sem("s_vp")
        s_ve = sem("s_ve")
        s_vw = sem("s_vw")
        s_nm = sem("s_nm")
        s_m0 = sem("s_m0")
        s_md = sem("s_md")
        s_mb = [sem(f"s_mb{i}") for i in range(2)]
        s_dm = sem("s_dm")
        s_dsel = sem("s_dsel")
        s_sc = sem("s_sc")
        s_cm = sem("s_cm")
        s_stp = sem("s_stp")
        s_st = sem("s_st")
        s_o = sem("s_o")
        s_oe = sem("s_oe")
        s_ones = sem("s_ones")
        s_xs = [sem(f"s_xs{i}") for i in range(NX)]
        s_xsp = sem("s_xsp")
        s_xse = sem("s_xse")
        s_h = sem("s_h")
        s_th = sem("s_th")
        s_uu = sem("s_uu")
        s_yp = sem("s_yp")
        s_ye = sem("s_ye")
        s_yst = [sem(f"s_yst{i}") for i in range(NX)]
        s_yg = [sem(f"s_yg{i}") for i in range(NPC)]
        s_norm = sem("s_norm")
        s_sy = sem("s_sy")
        s_id = sem("s_id")
        s_fin = sem("s_fin")
        s_finp = sem("s_finp")
        s_fina = sem("s_fina")
        s_sum = sem("s_sum")
        s_dummy = sem("s_dummy")
        s_gam = sem("s_gam")
        s_prod = sem("s_prod")
        s_out = sem("s_out")

        NSMALL = 11
        block = ctx.enter_context(nc.Block())

        @block.sync
        def _(sp):
            for i in range(XG):
                sp.dma_start(x_sb[:, i * TG:(i + 1) * TG, :], x_t[:, i * TG:(i + 1) * TG, :]).then_inc(s_x[i], 16)
            sp.wait_ge(s_small, 16 * NSMALL)
            for e in range(E):
                sp.dma_start(w1_sb[:, e, 0:H2], w1[e]).then_inc(s_w1, 16)
            sp.dma_start(w2_sb[:, :].rearrange("p (e c d) -> p e c d", e=E, c=HC),
                         w2.rearrange("e (c p) d -> p e c d", p=P)).then_inc(s_w2, 16)
            sp.dma_start(b2_sb[:, :, :], b2.partition_broadcast(P)).then_inc(s_w2, 16)
            sp.wait_ge(s_id, 3)
            sp.dma_start(xs_dram.rearrange("(n p) d -> p n d", p=P),
                         pad_row[:, :].unsqueeze(1).to_broadcast([P, NBLK, DW])).then_inc(s_fill, 16)

            sp.wait_ge(s_nm, 1)
            sp.dma_start(m_dram, nm[:, :]).then_inc(s_md, 16)
            sp.wait_ge(s_md, 16)
            for b in range(1, B):
                if b >= 3:
                    sp.wait_ge(s_dm, 2 * (b - 1))
                sp.dma_start(mb[:, b % 2, :, :], m_dram[NH * b:NH * (b + 1), :].partition_broadcast(P)).then_inc(s_mb[b % 2], 16)
            sp.wait_ge(s_scat, 16 * T)
            for c in range(NCH):
                if c >= NX:
                    sp.wait_ge(s_xsp, (c - NX + 1) * CH)
                    sp.wait_ge(s_yst[c % NX], 16 * CH * (c // NX))
                sp.dma_start(xs_sb[:, c % NX, :, :],
                             xs_dram[c * CH * P:(c + 1) * CH * P, :].rearrange("(n p) d -> p n d", p=P)).then_inc(s_xs[c % NX], 16)
            for i in range(NX):
                sp.wait_ge(s_yst[i], 16 * CH * len(range(i, NCH, NX)))
            for g in range(NPC):
                ts = slice(g * TP, (g + 1) * TP)
                sp.dma_start(yg[:, ts, :], y_t[:, ts, :]).then_inc(s_yg[g], 16)
            for g in range(NPC):
                ts = slice(g * TP, (g + 1) * TP)
                if g in POOL_PIECES:
                    sp.wait_ge(s_finp, POOL_PIECES.index(g) + 1)
                elif g in PE_PIECES:
                    sp.wait_ge(s_fina, PE_PIECES.index(g) + 1)
                else:
                    sp.wait_ge(s_fin, len([i for i in range(g + 1) if i not in POOL_PIECES + PE_PIECES]))
                sp.dma_start(out_t[:, ts, :], yg[:, ts, :]).then_inc(s_out, 16)
            sp.wait_ge(s_out, 16 * NPC)

        @block.gpsimd
        def _(pool):
            pool.memset(zeros[:, :], 0.0).then_inc(s_zero, 1)
            pool.memset(pad_row[:, 0:D], 0.0).then_inc(s_id, 1)
            pool.iota(pad_row[:, D:DW].bitcast(I32), [[0, 1]], base=NTOK, channel_multiplier=1).then_inc(s_id, 1)
            pool.iota(xw[:, :, D:DW].bitcast(I32), [[P, T], [0, 1]], base=0, channel_multiplier=1).then_inc(s_id, 1)
            pool.memset(ident[:, :], 0.0).then_inc(s_const, 1)
            pool.memset(block4[:, :], 1.0).then_inc(s_const, 1)
            pool.memset(head_mask[:, :, :], 1.0).then_inc(s_const, 1)
            pool.memset(tril[:, :], 1.0).then_inc(s_const, 1)
            pool.wait_ge(s_const, 4)
            pool.affine_select(out=ident[:, :], in_=ident[:, :], compare_op=ALU.not_equal, fill=1.0,
                               base=0, pattern=[[-1, P]], channel_multiplier=1).then_inc(s_const, 1)
            b4 = block4[:, :].rearrange("p (g o) -> p g o", o=4)
            pool.affine_select(out=b4, in_=b4, compare_op=ALU.is_ge, fill=0.0,
                               base=0, pattern=[[-4, P // 4], [0, 4]], channel_multiplier=1).then_inc(s_const, 1)
            pool.affine_select(out=head_mask[:, :, :], in_=head_mask[:, :, :], compare_op=ALU.is_ge, fill=0.0,
                               base=0, pattern=[[-DH, NH], [0, DA]], channel_multiplier=1).then_inc(s_const, 1)
            pool.affine_select(out=tril[:, :], in_=tril[:, :], compare_op=ALU.is_ge, fill=0.0,
                               base=-1, pattern=[[1, P]], channel_multiplier=-1).then_inc(s_const, 1)
            pool.wait_ge(s_const, 8)
            pool.affine_select(out=b4, in_=b4, compare_op=ALU.is_ge, fill=0.0,
                               base=3, pattern=[[4, P // 4], [0, 4]], channel_multiplier=-1).then_inc(s_const, 1)
            pool.affine_select(out=head_mask[:, :, :], in_=head_mask[:, :, :], compare_op=ALU.is_ge, fill=0.0,
                               base=DH - 1, pattern=[[DH, NH], [0, DA]], channel_multiplier=-1).then_inc(s_const, 1)
            pool.memset(ones_bf[:, :], 1.0).then_inc(s_const, 1)
            pool.iota(desc8[:, :], [[-1, E]], base=E, channel_multiplier=0,
                      allow_small_or_imprecise_dtypes=True).then_inc(s_const, 1)
            pool.iota(blk_start[:, :], [[P, NBLK]], base=0, channel_multiplier=0,
                      allow_small_or_imprecise_dtypes=True).then_inc(s_const, 1)
            pool.wait_ge(s_const, 13)
            pool.wait_ge(s_small, 16 * NSMALL)
            for n in range(3):
                pool.tensor_tensor(natbd[:, n, :].rearrange("p (g i) -> p g i", i=4),
                                   block4[:, :].rearrange("p (g i) -> p g i", i=4),
                                   nat[:, n, :].unsqueeze(1).to_broadcast([P, P // 4, 4]), ALU.mult).then_inc(s_nat, 1)
            pool.tensor_tensor(gates_w[:, :], gates_raw[:, 0:D], gates_raw[:, D:2 * D], ALU.add).then_inc(s_nat, 1)
            pool.wait_ge(s_nat, 4)
            pool.tensor_tensor(gates_raw[:, 0:D], gates_w[:, :], gates_raw[:, 2 * D:3 * D], ALU.add).then_inc(s_nat, 1)
            pool.tensor_scalar(gamma[:, :], gamma[:, :], 1.0, None, ALU.add).then_inc(s_prep, 1)
            pool.wait_ge(s_rs, 1)
            for t in range(3, T, 4):
                pool.tensor_scalar(xn[:, t, :], x_sb[:, t, :], rstd[:, t:t + 1], nmr[:, t:t + 1],
                                   ALU.mult, ALU.add).then_inc(s_xnp, 1)
            pool.memset(va[:, :, :, :, DH:DA], 1.0).then_inc(s_ones, 1)
            pool.memset(qm[:, :, :, :], 0.0).then_inc(s_ones, 1)

            def batch_masks(b):
                pool.wait_ge(s_ve, b + 1)
                pool.wait_ge(s_tm, 1)
                if b >= 2:
                    pool.wait_ge(s_stp, b - 1)
                pool.tensor_tensor(vw[:, b % 2, :, :], va[:, b % 2, 0, :, :],
                                   tm[:, 3, NH * b:NH * (b + 1)].unsqueeze(2).to_broadcast([P, NH, DA]),
                                   ALU.mult).then_inc(s_vw, 1)
                for k in range(2):
                    pool.wait_ge(s_dm, 2 * b + k + 1)
                    d = dm[:, b % 2, k, :, :]
                    pool.affine_select(out=d, in_=d, compare_op=ALU.is_ge, fill=0.0, base=0,
                                       pattern=[[0, NH], [1, P]], channel_multiplier=-1).then_inc(s_dsel, 1)

            for b in range(B):
                batch_masks(b)
                if b == 3:
                    pool.wait_ge(s_fill, 16)
                    pool.wait_ge(s_pos, 1)
                if b >= 3:
                    for t in range(3 * (b - 3), min(3 * (b - 2), T)):
                        pool.indirect_dma_start(xs_dram, bass.IndirectOffsetOnAxis(ap=pos[:, t:t + 1], axis=0),
                                                xw[:, t, :], None).then_inc(s_scat, 16)
            for j in range(NBLK):
                pool.wait_ge(s_ye, j + 1)
                pool.indirect_dma_start(y_dram, bass.IndirectOffsetOnAxis(
                    ap=xs_sb[:, j // CH % NX, j % CH, D:DW].bitcast(I32), axis=0),
                    ys_sb[:, j // CH % 2, j % CH, :], None, bounds_check=NTOK - 1, oob_is_err=False).then_inc(s_yst[j // CH % NX], 16)
                if j in GAMMA_AT:
                    g = GAMMA_AT.index(j)
                    b0, nb = GROUPS[g]
                    pool.wait_ge(s_norm, NSTEPS * (g + 1))
                    pool.tensor_tensor(u_all[:, 2 * b0:2 * (b0 + nb), :, 0:DH], sqs[g % 2],
                                       gamma[:, :].rearrange("p (h d) -> p h d", h=NH).unsqueeze(1).to_broadcast([P, GT, NH, DH]),
                                       ALU.mult).then_inc(s_gam, 1)
            for g in POOL_PIECES:
                y = yg[:, g * TP:(g + 1) * TP, :]
                pool.wait_ge(s_prod, g + 1)
                pool.tensor_tensor(y, y, x_sb[:, g * TP:(g + 1) * TP, :], ALU.add).then_inc(s_finp, 1)

        @block.scalar
        def _(act):
            for n, w in enumerate((wq, wk, wv)):
                act.dma_start(nat[:, n, :], w.rearrange("h o i -> (h o) i")).then_inc(s_small, 16)
            act.dma_start(rw_sb[:, 0:E], router_w).then_inc(s_small, 16)
            act.dma_start(gates_raw[0:NH, :], wf).then_inc(s_small, 16)
            act.dma_start(gates_raw[NH:2 * NH, :], wi).then_inc(s_small, 16)
            for n, v in ((0, router_b), (E, bf), (E + NH, bi)):
                act.dma_start(rb_sb[:, n:n + v.shape[0]], v.partition_broadcast(P)).then_inc(s_small, 16)
            act.dma_start(gamma[:, :], ln_w.partition_broadcast(P)).then_inc(s_small, 16)
            act.dma_start(b1_nat[:, :], b1.rearrange("e (c p) -> (e c) p", p=P)).then_inc(s_small, 16)
            act.wait_ge(s_zero, 1)
            act.activation(w_row[:, :], zeros[0:R, 0:P], ACT.Exp).then_inc(s_abs, 1)
            act.wait_ge(s_abs, 1)
            def xT_copy(q):
                act.wait_ge(s_xT, q + 1)
                act.activation(xnT[:, q * 512:(q + 1) * 512], xT_bank[q % 4][:, :], ACT.Copy).then_inc(s_xTe, 1)

            act.wait_ge(s_rs, 1)
            for q in range(T // 4 + 1):
                if q < T // 4:
                    t = 4 * q + 1
                    act.activation(xn[:, t, :], x_sb[:, t, :], ACT.Identity, scale=rstd[:, t:t + 1],
                                   bias=nmr[:, t:t + 1]).then_inc(s_xna, 1)
                if q >= 1 and q - 1 not in DVE_Q:
                    xT_copy(q - 1)
            act.wait_ge(s_gp, 1)
            act.activation(ga[:, :], bank[6][0:R, 0:S], ACT.Abs).then_inc(s_abs, 1)
            act.wait_ge(s_abs, 2)
            act.activation(gb[:, :], ga[:, :], ACT.Exp, scale=-1.0).then_inc(s_u, 1)
            act.wait_ge(s_w, 1)
            act.activation(lf[:, :], gc[:, :], ACT.Ln).then_inc(s_ln, 1)
            act.activation(ig[:, :], bank[6][R:2 * R, 0:S], ACT.Copy).then_inc(s_ig, 1)
            def evac_qk(b):
                act.wait_ge(s_qkp, b + 1)
                if b >= 2:
                    act.wait_ge(s_o, b - 1)
                for h in range(NH):
                    hs = slice(h * DH, (h + 1) * DH)
                    act.activation(qm[hs, b % 2, h, :], bank[0][hs, 0:S], ACT.Copy)
                act.activation(q1[:, b % 2, :], bank[0][:, P:S], ACT.Copy).then_inc(s_qke, 1)

            def decay(b):
                if b == 0:
                    act.wait_ge(s_m0, 1)
                else:
                    act.wait_ge(s_mb[b % 2], 16 * ((b + 1) // 2))
                act.wait_ge(s_tm, 1)
                if b >= 2:
                    act.wait_ge(s_cm, 2 * (b - 1))
                for k in range(2):
                    for h in range(NH):
                        src = mb[:, b % 2, h, k * P:(k + 1) * P]
                        if b == 0:
                            src = bank[3 if h < 2 else 6][:, (h % 2) * S + k * P:(h % 2) * S + (k + 1) * P]
                        last = act.activation(dm[:, b % 2, k, h, :], src, ACT.Exp,
                                              bias=tm[:, k, NH * b + h:NH * b + h + 1])
                    last.then_inc(s_dm, 1)

            def attention():
                evac_qk(0)
                act.activation(spare[:, :], zeros[:, 0:1], ACT.Exp).then_inc(s_dummy, 1)
                act.wait_ge(s_nm, 1)
                act.wait_ge(s_mm, 1)
                act.activation(w_row[:, :], gg[:, 0:P], ACT.Exp, bias=nm[:, P - 1:P]).then_inc(s_rows, 1)
                act.activation(eo_row[:, :], mm[:, P:S], ACT.Exp, scale=-1.0, bias=mm[:, P - 1:P]).then_inc(s_rows, 1)
                act.activation(fl_row[:, :], ga[:, :], ACT.Exp, scale=-1.0).then_inc(s_rows, 1)
                decay(0)
                for b in range(B):
                    if b + 1 < B:
                        evac_qk(b + 1)
                        decay(b + 1)

            act.wait_ge(s_ones, 2)
            attention()
            def copy_w(j):
                e = act.value_load(bexp_i[0:1, j:j + 1], min_val=0, max_val=E - 1)
                if j >= 3:
                    act.wait_ge(s_uu, j - 2)
                act.activation(wc[:, j % 3, HID:WB], w1_sb[:, bass.ds(e, 1), HID:WB], ACT.Copy).then_inc(s_wc, 1)

            act.wait_ge(s_w1, 16 * E)
            act.wait_ge(s_wts, 1)
            act.wait_ge(s_bexp, 1)
            def evac_xs(j):
                act.wait_ge(s_xsp, j + 1)
                if j >= 2:
                    act.wait_ge(s_h, j - 1)
                act.activation(xsT[:, j % 2, :], bank[4][:, 0:P], ACT.Copy).then_inc(s_xse, 1)

            copy_w(0)
            copy_w(1)
            evac_xs(0)
            for j in range(NBLK + 2):
                if j + 1 < NBLK:
                    evac_xs(j + 1)
                if 1 <= j < NBLK - 1:
                    copy_w(j + 1)
                if j < NBLK:
                    act.wait_ge(s_hg, j + 1)
                    act.wait_ge(s_wc, j + 1)
                    if j >= 2:
                        act.wait_ge(s_uu, j - 1)
                    for c in range(HC):
                        last = act.activation(sg[:, j % 2, c, :], bank[2 * (j % 2) + 1][:, c * P:(c + 1) * P], ACT.Sigmoid,
                                              bias=wc[:, j % 3, H2 + HC + c:H2 + HC + c + 1])
                    last.then_inc(s_th, 1)
                if j >= 2:
                    act.wait_ge(s_yb, j - 1)
                    if j >= 4:
                        act.wait_ge(s_ye, j - 3)
                    act.activation(sy[:, j % 2, :], yb[:, j % 2, :], ACT.Sigmoid).then_inc(s_sy, 1)
            for i, g in enumerate(PE_PIECES):
                act.wait_ge(s_sum, i + 1)
                act.activation(yg[:, g * TP:(g + 1) * TP, :], bank[i][:, :].rearrange("p (t d) -> p t d", d=D), ACT.Copy).then_inc(s_fina, 1)

        @block.vector
        def _(dve):
            chain = [0]

            def link(ins, fill=None):
                chain[0] += 1
                ins.then_inc(s_chain, 1)
                if fill:
                    nxt = next(fill, None)
                    if nxt is not None:
                        chain[0] += 1
                        nxt.then_inc(s_chain, 1)
                dve.wait_ge(s_chain, chain[0])

            def rsqrt_steps(v, n):
                a, b, y, y2 = ra[:, 0:n], rb_[:, 0:n], ry[:, 0:n], ry2[:, 0:n]
                yield dve.tensor_scalar(a.bitcast(I32), v.bitcast(I32), 1, None, ALU.logical_shift_right)
                yield dve.tensor_scalar(y.bitcast(I32), a.bitcast(I32), -1.0, float(0x5F3759DF), ALU.mult, ALU.add)
                for _ in range(3):
                    yield dve.tensor_tensor(a, y, y, ALU.mult)
                    yield dve.scalar_tensor_tensor(b, a, -0.5, v, ALU.mult, ALU.mult)
                    yield dve.scalar_tensor_tensor(y2, b, 1.5, y, ALU.add, ALU.mult)
                    y, y2 = y2, y
                return y

            for t in range(T):
                if t % TG == 0:
                    dve.wait_ge(s_x[t // TG], 16)
                last = dve.bn_stats(stats[:, t, :], x_sb[:, t, :])
            link(last)
            for t in range(T):
                last = dve.bn_aggr(mv[:, t, :], stats[:, t, :])
            link(last)
            link(dve.tensor_scalar(veps[:, 0:T], mv[:, :, 1], EPS_LN, None, ALU.add))
            y = ry2[:, 0:T]
            for ins in rsqrt_steps(veps[:, 0:T], T):
                link(ins)
            link(dve.tensor_copy(rstd[:, :], y))
            dve.scalar_tensor_tensor(nmr[:, :], mv[:, :, 0], -1.0, rstd[:, :], ALU.mult, ALU.mult).then_inc(s_rs, 1)
            dve.wait_ge(s_rs, 1)

            def xT_copy(q):
                dve.wait_ge(s_xT, q + 1)
                dve.tensor_copy(xnT[:, q * 512:(q + 1) * 512], xT_bank[q % 4][:, :]).then_inc(s_xTd, 1)

            for q in range(T // 4 + 1):
                if q < T // 4:
                    for t in (4 * q, 4 * q + 2):
                        dve.tensor_scalar(xn[:, t, :], x_sb[:, t, :], rstd[:, t:t + 1], nmr[:, t:t + 1],
                                          ALU.mult, ALU.add).then_inc(s_xn, 1)
                if q == 0:
                    dve.wait_ge(s_wT, 1)
                    dve.tensor_copy(rw_sb[:, E:NL], bank[4][:, 2 * P:2 * P + 2 * NH]).then_inc(s_gw, 1)
                if q >= 1 and q - 1 in DVE_Q:
                    xT_copy(q - 1)
            dve.wait_ge(s_prep, 1)
            dve.tensor_scalar(wqk[:, :], bank[4][:, 0:P], float(DH) ** -0.5, None, ALU.mult)
            link(dve.tensor_copy(wbd[:, :], bank[4][:, P:2 * P]))
            link(dve.tensor_reduce(vmean[:, :], wbd[:, :].rearrange("p (h d) -> p h d", h=NH), AX.X, ALU.add))
            link(dve.tensor_scalar(vmean[:, :], vmean[:, :], -1.0 / DH, None, ALU.mult))
            dve.tensor_tensor(wvc[:, :].rearrange("p (h d) -> p h d", h=NH),
                              wbd[:, :].rearrange("p (h d) -> p h d", h=NH),
                              vmean[:, :].unsqueeze(2).to_broadcast([P, NH, DH]), ALU.add)
            dve.tensor_copy(w1_sb[:, :, H2:WB], bank[5][:, 0:E * (WB - H2)].rearrange("p (e c) -> p e c", e=E)).then_inc(s_wts, 1)

            dve.wait_ge(s_lg, 1)
            for k in range(2):
                dve.tensor_tensor(gtok[:, k, :, :, :].rearrange("p y b h -> p b y h"),
                                  bank[2][:, :].rearrange("p (b k c) -> p k b c", k=2, c=NL)[:, k, :, E:NL]
                                  .rearrange("p b (y h) -> p b y h", h=NH),
                                  rb_sb[:, E:NL].rearrange("p (y h) -> p y h", h=NH).unsqueeze(1).to_broadcast([P, B, 2, NH]),
                                  ALU.add).then_inc(s_gt, 1)


            def route():
                yield dve.tensor_tensor(lg[:, :, :], bank[2][:, :].rearrange("p (t c) -> p t c", c=NL)[:, :, 0:E],
                                        rb_sb[:, 0:E].unsqueeze(1).to_broadcast([P, T, E]), ALU.add)
                yield dve.tensor_reduce(rmax[:, :], lg[:, :, :], AX.X, ALU.max)
                yield dve.tensor_tensor(r1[:, :, :], lg[:, :, :], rmax[:, :].unsqueeze(2).to_broadcast([P, T, E]), ALU.is_equal)
                yield dve.tensor_tensor(lg[:, :, :], r1[:, :, :], desc8[:, :].unsqueeze(1).to_broadcast([P, T, E]), ALU.mult)
                yield dve.tensor_reduce(rmax[:, :], lg[:, :, :], AX.X, ALU.max)

            router = route()
            for _ in range(2):
                link(next(router))
            dve.wait_ge(s_u, 1)
            link(dve.tensor_scalar(gc[:, :], gb[:, :], 1.0, None, ALU.add))
            dve.scalar_tensor_tensor(gb[:, :], gc[:, :], -1.0, gb[:, :], ALU.add, ALU.subtract).then_inc(s_w, 1)
            for _ in range(2):
                link(next(router))

            dve.wait_ge(s_ln, 1)
            dve.wait_ge(s_w, 1)
            link(dve.tensor_tensor(gc[:, :], gb[:, :], lf[:, :], ALU.subtract), router)
            dve.scalar_tensor_tensor(lf[:, :], bank[6][0:R, 0:S], 0.0, gc[:, :], ALU.min, ALU.add).then_inc(s_chain, 1)
            chain[0] += 1
            dve.tensor_tensor(oh[:, :, :].rearrange("p e t -> p t e"), rmax[:, :].unsqueeze(2).to_broadcast([P, T, E]),
                              desc8[:, :].unsqueeze(1).to_broadcast([P, T, E]), ALU.is_equal).then_inc(s_oh, 1)
            dve.wait_ge(s_chain, chain[0])
            link(dve.tensor_tensor_scan(fsum[:, :], lf[:, :], zeros[0:R, :], 0.0, ALU.add, ALU.add))
            dve.wait_ge(s_ig, 1)

            def counts():
                dve.wait_ge(s_cnt, 1)
                yield dve.tensor_copy(cnt[:, :, :], bank[7][:, 0:E * T].rearrange("p (e t) -> p e t", e=E))
                yield dve.tensor_copy(pos3[:, :, :], bank[7][:, E * T:2 * E * T].rearrange("p (e t) -> p e t", e=E))

            fill = counts()
            link(dve.tensor_tensor(gg[:, :], ig[:, :], fsum[:, :], ALU.subtract))
            link(dve.tensor_tensor_scan(mm[:, :], gg[:, :], gg[:, :], -BIG, ALU.max, ALU.max))
            dve.tensor_scalar(nm[:, :], mm[:, :], -1.0, None, ALU.mult).then_inc(s_nm, 1)
            dve.tensor_tensor(ga[:, :], fsum[:, :], mm[:, :], ALU.add).then_inc(s_mm, 1)
            for ins in fill:
                link(ins)
            dve.wait_ge(s_tmp, 1)
            dve.tensor_copy(tm[:, :, :], bank[2][:, 0:6 * R].rearrange("p (n r) -> p n r", n=6)).then_inc(s_tm, 1)
            dve.wait_ge(s_tm, 1)
            dve.wait_ge(s_ones, 2)

            def routing(part):
                flat = "p e t -> p (e t)"
                if part == 0:
                    link(dve.tensor_tensor_scan(csum[:, :, :].rearrange(flat), cnt[:, :, :].rearrange(flat),
                                                zeros[:, 0:E * T], 0.0, ALU.add, ALU.add))
                    link(dve.tensor_reduce(ecount[:, :], cnt[:, :, :], AX.X, ALU.add))
                if part == 1:
                    link(dve.tensor_scalar(ecount_i[:, :], ecount[:, :], float(P - 1), None, ALU.add))
                    link(dve.tensor_scalar(epad_i[:, :], ecount_i[:, :], 7, 7, ALU.logical_shift_right, ALU.logical_shift_left))
                    link(dve.tensor_copy(epad[:, :], epad_i[:, :]))
                    link(dve.tensor_tensor_scan(eend[:, :], epad[:, :], zeros[:, 0:E], 0.0, ALU.add, ALU.add))
                    link(dve.tensor_tensor(edelta[:, :], eend[:, :], epad[:, :], ALU.subtract))
                    link(dve.tensor_tensor(edelta[:, :], edelta[:, :], csum[:, :, T - 1], ALU.subtract))
                    link(dve.tensor_tensor(edelta[:, :], edelta[:, :], ecount[:, :], ALU.add))
                if part == 2:
                    link(dve.tensor_tensor(csum[:, :, :], csum[:, :, :], cnt[:, :, :], ALU.subtract))
                    link(dve.tensor_tensor(csum[:, :, :], csum[:, :, :], edelta[:, :].unsqueeze(2).to_broadcast([P, E, T]), ALU.add))
                    link(dve.tensor_tensor(pos3[:, :, :], pos3[:, :, :], csum[:, :, :], ALU.add))
                    link(dve.tensor_tensor(pos3[:, :, :], pos3[:, :, :], oh[:, :, :], ALU.mult))
                    link(dve.tensor_reduce(posf[:, :], pos3[:, :, :].rearrange("p e t -> p t e"), AX.X, ALU.add))
                    dve.tensor_copy(pos[:, :], posf[:, :]).then_inc(s_pos, 1)
                if part == 3:
                    link(dve.tensor_tensor(bcmp[:, :, :], blk_start[:, :].unsqueeze(2).to_broadcast([P, NBLK, E]),
                                           eend[:, :].unsqueeze(1).to_broadcast([P, NBLK, E]), ALU.is_ge))
                    link(dve.tensor_reduce(bexp[:, :], bcmp[:, :, :], AX.X, ALU.add))
                    link(dve.tensor_scalar(bexp[:, :], bexp[:, :], float(E - 1), None, ALU.min))
                    dve.tensor_copy(bexp_i[:, :], bexp[:, :]).then_inc(s_bexp, 1)
    
            def copy_w(j):
                e = dve.value_load(bexp_i[0:1, j:j + 1], min_val=0, max_val=E - 1)
                if j >= 3:
                    dve.wait_ge(s_h, j - 2)
                dve.tensor_copy(wc[:, j % 3, 0:HID], w1_sb[:, bass.ds(e, 1), 0:HID]).then_inc(s_wv, 1)

            def evac_v(b):
                dve.wait_ge(s_vp, b + 1)
                if b >= 2:
                    dve.wait_ge(s_o, b - 1)
                    dve.wait_ge(s_vw, b - 1)
                dve.tensor_copy(va[:, b % 2, :, :, 0:DH],
                                bank[1][:, 0:2 * P].rearrange("p (k h d) -> p k h d", k=2, d=DH)).then_inc(s_ve, 1)

            def scores(b):
                for k in range(2):
                    dve.wait_ge(s_sc, 2 * b + k + 1)
                    dve.wait_ge(s_dsel, 2 * b + k + 1)
                    if b >= 2:
                        dve.wait_ge(s_o, b - 1)
                    dve.tensor_tensor(cm[:, b % 2, k, :, :], dm[:, b % 2, k, :, :],
                                      bank[4 + k][:, :].rearrange("p (h s) -> p h s", h=NH), ALU.mult).then_inc(s_cm, 1)

            def state(b):
                dve.wait_ge(s_stp, b + 1)
                if b >= 2:
                    dve.wait_ge(s_o, b - 1)
                dve.tensor_tensor(st[:, b % 2, :, :], head_mask[:, :, :],
                                  bank[6][:, 0:NH * DA].rearrange("p (h d) -> p h d", h=NH), ALU.mult).then_inc(s_st, 1)

            def outputs(b):
                dve.wait_ge(s_o, b + 1)
                hd = "p (h d) -> p h d"
                n = NH * DA
                dve.tensor_copy(u_all[:, 2 * b, :, :], bank[7][:, 0:n].rearrange(hd, h=NH))
                link(dve.tensor_tensor(ot[:, :, :], bank[7][:, 2 * n:3 * n].rearrange(hd, h=NH),
                                       tm[:, 2, NH * b:NH * (b + 1)].unsqueeze(2).to_broadcast([P, NH, DA]), ALU.mult))
                dve.tensor_tensor(u_all[:, 2 * b + 1, :, :], ot[:, :, :], bank[7][:, n:2 * n].rearrange(hd, h=NH),
                                  ALU.add).then_inc(s_oe, 1)

            def attention():
                evac_v(0)
                for b in range(B):
                    scores(b)
                    state(b)
                    if b + 1 < B:
                        evac_v(b + 1)
                    else:
                        dve.wait_ge(s_w1, 16 * E)
                        dve.wait_ge(s_bexp, 1)
                        copy_w(0)
                    outputs(b)
                    if b < 4:
                        routing(b)

            def normalise(g):
                b0, nb = GROUPS[g]
                nt = 2 * nb
                n = nt * NH
                uv = u_all[:, 2 * b0:2 * b0 + nt, :, 0:DH]
                rs = u_all[:, 2 * b0:2 * b0 + nt, :, DH]
                dve.wait_ge(s_oe, b0 + nb)
                sq = sqs[g % 2]
                halves = [(i * nt // 2, (i + 1) * nt // 2) for i in range(2)]
                if g >= 2:
                    dve.wait_ge(s_gam, g - 1)
                for a, b in halves:
                    yield dve.tensor_tensor(sq[:, a:b, :, :], uv[:, a:b, :, :], uv[:, a:b, :, :], ALU.mult)
                for a, b in halves:
                    yield dve.tensor_reduce(ssum[:, a * NH:b * NH], sq[:, a:b, :, :], AX.X, ALU.add)
                d4 = den[:, 0:n].rearrange("p (b k h) -> p b k h", k=2, h=NH)
                yield dve.scalar_tensor_tensor(den[:, 0:n].rearrange("p (t h) -> p t h", h=NH), rs, -1.0, rs, ALU.mult, ALU.max)
                yield dve.tensor_tensor(d4, d4, tm[:, 4:6, b0 * NH:(b0 + nb) * NH].rearrange("p k (b h) -> p b k h", h=NH), ALU.max)
                yield dve.tensor_scalar(den[:, 0:n], den[:, 0:n], EPS_N, None, ALU.add)
                yield dve.reciprocal(rden[:, 0:n], den[:, 0:n])
                yield dve.scalar_tensor_tensor(ssum[:, 0:n], ssum[:, 0:n], 1.0 / DH, rden[:, 0:n], ALU.mult, ALU.mult)
                yield dve.tensor_tensor(ssum[:, 0:n], ssum[:, 0:n], rden[:, 0:n], ALU.mult)
                yield dve.tensor_scalar(veps[:, 0:n], ssum[:, 0:n], EPS_LN, None, ALU.add)
                y = yield from rsqrt_steps(veps[:, 0:n], n)
                yield dve.tensor_tensor(coef[:, 0:n], y, rden[:, 0:n], ALU.mult)
                for a, b in halves:
                    yield dve.tensor_tensor(sq[:, a:b, :, :], uv[:, a:b, :, :],
                                            coef[:, a * NH:b * NH].rearrange("p (t h) -> p t h", h=NH).unsqueeze(3).to_broadcast([P, b - a, NH, DH]),
                                            ALU.mult)

            def normalise_all(groups):
                for g in groups:
                    yield from normalise(g)

            def step(steps, count=1):
                for _ in range(count):
                    dve.wait_ge(s_norm, norms[0])
                    ins = next(steps, None)
                    if ins is None:
                        return False
                    norms[0] += 1
                    ins.then_inc(s_norm, 1)
                return True

            norms = [0]

            def finish():
                for g in range(NPC):
                    ts = slice(g * TP, (g + 1) * TP)
                    y = yg[:, ts, :]
                    hd = "p t (h d) -> p t h d"
                    dve.wait_ge(s_yg[g], 16)
                    dve.wait_ge(s_gam, len(GROUPS))
                    dve.tensor_tensor(y.rearrange(hd, h=NH), y.rearrange(hd, h=NH), u_all[:, ts, :, 0:DH],
                                      ALU.mult).then_inc(s_prod, 1)
                    if g not in POOL_PIECES + PE_PIECES:
                        dve.wait_ge(s_prod, g + 1)
                        dve.tensor_tensor(y, y, x_sb[:, ts, :], ALU.add).then_inc(s_fin, 1)

            attention()

            def product(j):
                dve.wait_ge(s_th, j + 1)
                dve.wait_ge(s_h, j + 1)
                if j >= 2:
                    dve.wait_ge(s_yp, j - 1)
                for c in range(HC):
                    last = dve.scalar_tensor_tensor(uT[:, j % 2, c, :], bank[2 * (j % 2)][:, c * P:(c + 1) * P],
                                                    wc[:, j % 3, H2 + c:H2 + c + 1], sg[:, j % 2, c, :], ALU.add, ALU.mult)
                last.then_inc(s_uu, 1)

            def add_bias(j):
                e = dve.value_load(bexp_i[0:1, j:j + 1], min_val=0, max_val=E - 1)
                dve.wait_ge(s_yp, j + 1)
                if j >= 2:
                    dve.wait_ge(s_ye, j - 1)
                dve.tensor_tensor(yb[:, j % 2, :].unsqueeze(1), bank[6 + j % 2][:, 0:D].unsqueeze(1), b2_sb[:, bass.ds(e, 1), :], ALU.add).then_inc(s_yb, 1)

            def silu(j):
                dve.wait_ge(s_yb, j + 1)
                dve.wait_ge(s_sy, j + 1)
                c = j // CH - 2
                if c >= 0 and j % CH == 0:
                    dve.wait_ge(s_yst[c % NX], 16 * CH * (c // NX + 1))
                dve.tensor_tensor(ys_sb[:, (j // CH) % 2, j % CH, :], sy[:, j % 2, :], yb[:, j % 2, :], ALU.mult).then_inc(s_ye, 1)

            dve.wait_ge(s_w2, 32)
            normals = normalise_all(range(len(GROUPS)))
            for j in range(NBLK + 2):
                if j + 1 < NBLK:
                    copy_w(j + 1)
                    step(normals)
                if j < NBLK:
                    product(j)
                    step(normals)
                if 1 <= j <= NBLK:
                    add_bias(j - 1)
                if j >= 2:
                    silu(j - 2)
                step(normals)
            while step(normals):
                pass

            finish()

        @block.tensor
        def _(pe):
            def evacuated(q):
                if q in DVE_Q:
                    pe.wait_ge(s_xTd, DVE_Q.index(q) + 1)
                else:
                    pe.wait_ge(s_xTe, len([i for i in range(q + 1) if i not in DVE_Q]))

            def transposes(q):
                pe.wait_ge(s_xn, 2 * (q + 1))
                pe.wait_ge(s_xna, q + 1)
                pe.wait_ge(s_xnp, q + 1)
                if q >= 4:
                    evacuated(q - 4)
                for i in range(4):
                    last = pe.transpose(xT_bank[q % 4][:, i * P:(i + 1) * P], xn[:, 4 * q + i, :], ident[:, :])
                last.then_inc(s_xT, 1)

            def logits(q):
                evacuated(q)
                for t in range(4 * q, 4 * q + 4):
                    last = pe.matmul(bank[2][:, t * NL:(t + 1) * NL], xnT[:, t * P:(t + 1) * P], rw_sb[:, :],
                                     start=True, stop=True)
                if q == T // 4 - 1:
                    last.then_inc(s_lg, 1)

            def keep_warm(n, b):
                for _ in range(n):
                    pe.matmul(bank[b][:, 0:S], zeros[:, 0:P], zeros[:, :], start=True, stop=True)

            pe.wait_ge(s_zero, 1)
            pe.wait_ge(s_x[XG - 1], 16)
            keep_warm(6, 7)
            pe.wait_ge(s_const, 13)
            pe.wait_ge(s_small, 16 * NSMALL)
            pe.wait_ge(s_nat, 5)
            pe.matmul(bank[4][:, 0:P], natbd[:, 0, :], natbd[:, 1, :], start=True, stop=True)
            pe.transpose(bank[4][:, P:2 * P], natbd[:, 2, :], ident[:, :])
            pe.transpose(bank[4][:, 2 * P:2 * P + 2 * NH], gates_raw[:, 0:D], ident[0:2 * NH, 0:2 * NH])
            pe.transpose(bank[5][:, 0:E * (WB - H2)], b1_nat[:, :], ident[0:E * (WB - H2), 0:E * (WB - H2)]).then_inc(s_wT, 1)
            keep_warm(2, 7)
            pe.wait_ge(s_gw, 1)
            transposes(0)
            transposes(1)
            for q in range(2, T // 4):
                transposes(q)
                logits(q - 2)
            logits(T // 4 - 2)
            logits(T // 4 - 1)
            for k in range(2):
                pe.wait_ge(s_gt, k + 1)
                last = pe.transpose(bank[6][:, k * P:(k + 1) * P], gtok[:, k, :, :, :].rearrange("p y b h -> p (y b h)"), ident[:, :])
            last.then_inc(s_gp, 1)
            def project(b):
                xb = xnT[:, b * S:(b + 1) * S]
                if b >= 1:
                    pe.wait_ge(s_qke, b)
                pe.matmul(bank[0][:, 0:S], wqk[:, :], xb, start=True, stop=True).then_inc(s_qkp, 1)
                if b >= 1:
                    pe.wait_ge(s_ve, b)
                for k in range(2):
                    last = pe.matmul(bank[1][:, k * P:(k + 1) * P], xnT[:, b * S + k * P:b * S + (k + 1) * P], wvc[:, :],
                                     start=True, stop=True)
                last.then_inc(s_vp, 1)

            def rowsT(j):
                if j % CH == 0:
                    pe.wait_ge(s_xs[j // CH % NX], 16 * (j // CH // NX + 1))
                if j >= 1:
                    pe.wait_ge(s_xse, j)
                pe.transpose(bank[4][:, 0:P], xs_sb[:, j // CH % NX, j % CH, 0:D], ident[:, :]).then_inc(s_xsp, 1)

            def scores(b, tiles=range(2)):
                pe.wait_ge(s_qke, b + 1)
                if b >= 1:
                    pe.wait_ge(s_cm, 2 * b)
                for k in tiles:
                    pe.matmul(bank[4 + k][:, :], xnT[:, b * S + k * P:b * S + (k + 1) * P],
                              qm[:, b % 2, :, k * P:(k + 1) * P], start=True, stop=True).then_inc(s_sc, 1)

            def attention():
                scores(0, (0,))
                idr = ident[0:R, 0:R]
                pe.wait_ge(s_nm, 1)
                for h in range(NH):
                    last = pe.matmul(bank[3 if h < 2 else 6][:, (h % 2) * S:(h % 2 + 1) * S],
                                     idr[:, h:h + 1].to_broadcast([R, P]), nm[:, :], start=True, stop=True)
                last.then_inc(s_m0, 1)
                pe.wait_ge(s_rows, 3)
                for n, v in enumerate((gg[:, 0:P], gg[:, P:S], eo_row[:, :], w_row[:, :], fl_row[:, 0:P], fl_row[:, P:S])):
                    last = pe.transpose(bank[2][:, n * R:(n + 1) * R], v, idr)
                last.then_inc(s_tmp, 1)
                scores(0, (1,))
                keep_warm(1, 0)
                pe.wait_ge(s_tm, 1)
                pe.wait_ge(s_dm, 2)
                for b in range(B):
                    if b >= 1:
                        scores(b)
                    pe.wait_ge(s_vw, b + 1)
                    if b >= 1:
                        pe.wait_ge(s_st, b)
                    pe.matmul(bank[6][:, 0:NH * DA], xn[:, 2 * b, :],
                              vw[:, b % 2, :, :].rearrange("p h d -> p (h d)"), start=True, stop=True).then_inc(s_stp, 1)
                    if b + 1 < B:
                        project(b + 1)
                    if b >= 1:
                        pe.wait_ge(s_oe, b)
                    if b + 1 == B:
                        keep_warm(3, 0)
                    if b == 0:
                        keep_warm(2, 3)
                    n = NH * DA
                    for k in range(2):
                        pe.wait_ge(s_cm, 2 * b + k + 1)
                        for h in range(NH):
                            pe.matmul(bank[7][:, k * n + h * DA:k * n + (h + 1) * DA], cm[:, b % 2, k, h, :],
                                      va[:, b % 2, k, h, :], start=True, stop=True)
                    if b + 1 == B:
                        rowsT(0)
                    pe.wait_ge(s_st, b + 1)
                    pe.matmul(bank[7][:, 2 * n:3 * n], q1[:, b % 2, :],
                              st[:, b % 2, :, :].rearrange("p h d -> p (h d)"), start=True, stop=True).then_inc(s_o, 1)

            pe.wait_ge(s_wts, 1)
            project(0)
            keep_warm(2, 7)
            pe.wait_ge(s_oh, 1)
            ohf = oh[:, :, :].rearrange("p e t -> p (e t)")
            pe.matmul(bank[7][:, 0:E * T], ones_bf[:, :], ohf, start=True, stop=True)
            pe.matmul(bank[7][:, E * T:2 * E * T], tril[:, :], ohf, start=True, stop=True).then_inc(s_cnt, 1)
            pe.wait_ge(s_ones, 2)
            attention()

            def hidden(j):
                pe.wait_ge(s_xse, j + 1)
                pe.wait_ge(s_wc, j + 1)
                if j >= 2:
                    pe.wait_ge(s_uu, j - 1)
                for k, done in ((1, s_hg), (0, s_h)):
                    if k == 0:
                        pe.wait_ge(s_wv, j + 1)
                    for c in range(HC):
                        m = (k * HC + c) * P
                        last = pe.matmul(bank[2 * (j % 2) + k][:, c * P:(c + 1) * P], wc[:, j % 3, m:m + P],
                                         xsT[:, j % 2, :], start=True, stop=True)
                    last.then_inc(done, 1)

            def down(j, e):
                pe.wait_ge(s_uu, j + 1)
                if j >= 2:
                    pe.wait_ge(s_yb, j - 1)
                for c in range(HC):
                    last = pe.matmul(bank[6 + j % 2][:, 0:D], uT[:, j % 2, c, :], w2_sb[:, bass.ds(e * (HC * D) + c * D, D)],
                                     start=(c == 0), stop=(c == HC - 1))
                last.then_inc(s_yp, 1)

            pe.wait_ge(s_w2, 32)
            pe.wait_ge(s_bexp, 1)
            for j in range(NBLK + 1):
                if j + 1 < NBLK:
                    rowsT(j + 1)
                if j < NBLK:
                    hidden(j)
                if j >= 1:
                    down(j - 1, pe.value_load(bexp_i[0:1, j - 1:j], min_val=0, max_val=E - 1))

            pe.wait_ge(s_uu, NBLK)
            for i, g in enumerate(PE_PIECES):
                pe.matmul(bank[i][:, :], ident[:, :], x_sb[:, g * TP:(g + 1) * TP, :], start=True, stop=False)
            keep_warm(9, 4)
            for i, g in enumerate(PE_PIECES):
                pe.wait_ge(s_prod, g + 1)
                pe.matmul(bank[i][:, :], ident[:, :], yg[:, g * TP:(g + 1) * TP, :], start=False, stop=True).then_inc(s_sum, 1)


_INS = ["L0_attn_x", "L0_attn_wq", "L0_attn_wk", "L0_attn_wv", "L0_attn_wi", "L0_attn_bi", "L0_attn_wf", "L0_attn_bf",
        "L0_attn_ln_w", "L0_ffn_router_w", "L0_ffn_router_b", "L0_ffn_w1", "L0_ffn_b1", "L0_ffn_w2", "L0_ffn_b2"]


def kernel(**inputs):
    import numpy as _np
    import concourse.bacc as _bacc
    from concourse import mybir as _mybir
    from concourse.bass_utils import run_bass_kernel_spmd as _run

    nc = _bacc.Bacc("TRN2", target_bir_lowering=False, num_devices=1)
    arrays, args = {}, []
    for name in _INS:
        a = _np.ascontiguousarray(inputs[name])
        arrays[f"in_{name}"] = a
        args.append(nc.dram_tensor(f"in_{name}", a.shape, _mybir.dt.from_np(a.dtype), kind="ExternalInput").ap())
    shape = tuple(inputs["L0_attn_x"].shape)
    out = nc.dram_tensor("out_x", shape, _mybir.dt.float32, kind="ExternalOutput").ap()
    mlstm_moe_block(nc, *args, out)
    r = _run(nc, [arrays], core_ids=[0])
    return r.results[0]["out_x"]
```
